# Optimizing a Trainium2 kernel written in Bass

```python
import numpy as np
import jax
import jax.numpy as jnp

def _softmax(x, axis=-1):
    return jax.nn.softmax(x, axis=axis)

def _gelu(x):
    return jax.nn.gelu(x, approximate=True)

def _silu(x):
    return jax.nn.silu(x)

def _sigmoid(x):
    return jax.nn.sigmoid(x)

def _layernorm(x, axis=-1, eps=1e-05):
    m = jnp.mean(x, axis=axis, keepdims=True)
    v = jnp.var(x, axis=axis, keepdims=True)
    return (x - m) / jnp.sqrt(v + eps)

def _scatter_add(tgt, idx, src, axis=0):
    return tgt.at[idx].add(src)

def _segment_sum(src, seg, n):
    return jax.ops.segment_sum(src, seg, n)
kernel_name = 'mk_decoder_postln_d1_seqx_r4_02fa18'

def setup_inputs(seed: int=0):
    np.random.seed(seed)
    _w = jnp.asarray

    def _rec_inputs():
        import jax
        import jax.numpy as jnp
        _rk = jax.random.key(seed)
        x = 6.313e-05 + 0.9998 * jax.random.normal(jax.random.fold_in(_rk, 1), (32, 256, 256), jnp.float32)
        _lenS = 256 - jax.random.randint(jax.random.fold_in(_rk, 7), (32,), 0, max(1, 256 // 4) + 1, jnp.int32)
        _lenS2 = 77 - jax.random.randint(jax.random.fold_in(_rk, 8), (32,), 0, max(1, 77 // 4) + 1, jnp.int32)
        _ctx_1024P = jax.random.normal(jax.random.fold_in(_rk, 11), (32, 16, 256), jnp.float32)
        _ctx_1024c = jax.random.dirichlet(jax.random.fold_in(_rk, 511), 0.3 * jnp.ones((16,), jnp.float32), (32, 77))
        _ctx_1024t = jnp.einsum('bsk,bkd->bsd', _ctx_1024c, _ctx_1024P)
        _ctx_1024t = _ctx_1024t * jax.lax.rsqrt(jnp.mean(jnp.square(_ctx_1024t)) + 1e-12) * 0.953939
        ctx_1024 = -0.000214406 + 1.00034 * (_ctx_1024t + 0.3 * jax.random.normal(jax.random.fold_in(_rk, 611), (32, 77, 256), jnp.float32))
        return (x, ctx_1024)
    x, ctx_1024 = _rec_inputs()

    def _L0_attn_setup():
        import jax, jax.numpy as jnp
        import numpy as np
        N_HEAD = 16
        key = jax.random.key(seed)
        k1, k2, k3, k4, k5 = jax.random.split(key, 5)
        B, T, C = (8, 512, 256)
        hs = C // N_HEAD
        return {'ids': jax.random.normal(k1, (B, T, C), dtype=jnp.float32), 'qkv_w': jax.random.normal(k2, (3 * hs, C), dtype=jnp.float32) * C ** (-0.5), 'qkv_b': jax.random.normal(k3, (3 * hs,), dtype=jnp.float32) * 0.02, 'proj_w': jax.random.normal(k4, (C, C), dtype=jnp.float32) * C ** (-0.5), 'proj_b': jax.random.normal(k5, (C,), dtype=jnp.float32) * 0.02}
    _L0_attn_all = _L0_attn_setup()
    _L0_attn_in = {k: v for k, v in _L0_attn_all.items() if k in ('qkv_w', 'qkv_b', 'proj_w', 'proj_b')}
    del _L0_attn_all

    def _L0_xattn_setup():
        import jax, jax.numpy as jnp
        import numpy as np
        from jax import lax
        BIG = jnp.float32(1e+30)

        def _pairwise_euclidean(a, b):
            aa = jnp.sum(a * a, axis=-1)[:, None]
            bb = jnp.sum(b * b, axis=-1)[None, :]
            ab = a @ b.T
            return jnp.sqrt(jnp.maximum(aa + bb - 2.0 * ab, 0.0))

        def _dtw_cost(D):
            row0 = jnp.cumsum(D[0])

            def row_step(prev_row, d_row):
                first = d_row[0] + prev_row[0]

                def col_step(left, inp):
                    d_ij, up, diag = inp
                    r = d_ij + jnp.minimum(jnp.minimum(up, left), diag)
                    return (r, r)
                _, rest = lax.scan(col_step, first, (d_row[1:], prev_row[1:], prev_row[:-1]))
                row = jnp.concatenate([first[None], rest])
                return (row, row)
            _, rows = lax.scan(row_step, row0, D[1:])
            return jnp.concatenate([row0[None], rows], axis=0)

        def _backtrack(R, T1, T2):
            L = T1 + T2 - 1

            def step(carry, _):
                i, j, done = carry
                valid = jnp.logical_not(done)
                cd = jnp.where((i > 0) & (j > 0), R[jnp.maximum(i - 1, 0), jnp.maximum(j - 1, 0)], BIG)
                cu = jnp.where(i > 0, R[jnp.maximum(i - 1, 0), j], BIG)
                cl = jnp.where(j > 0, R[i, jnp.maximum(j - 1, 0)], BIG)
                choice = jnp.argmin(jnp.stack([cd, cu, cl]))
                ni = jnp.where(choice <= 1, i - 1, i)
                nj = jnp.where((choice == 0) | (choice == 2), j - 1, j)
                at_origin = (i == 0) & (j == 0)
                ni = jnp.where(at_origin, 0, ni)
                nj = jnp.where(at_origin, 0, nj)
                return ((ni, nj, done | at_origin), (i, j, valid))
            init = (jnp.int32(T1 - 1), jnp.int32(T2 - 1), jnp.bool_(False))
            _, (i_idx, j_idx, valid) = lax.scan(step, init, None, length=L)
            return (i_idx, j_idx, valid)

        def _align_one(small, large):
            T_small, d = small.shape
            T_large = large.shape[0]
            D = _pairwise_euclidean(small, large)
            R = _dtw_cost(D)
            i_idx, j_idx, valid = _backtrack(R, T_small, T_large)
            contrib = small[i_idx] * valid[:, None].astype(small.dtype)
            expanded = jnp.zeros((T_large, d), dtype=small.dtype).at[j_idx].add(contrib)
            return expanded
        key = jax.random.key(seed)
        k1, k2 = jax.random.split(key)
        teacher = jax.random.normal(k1, (16, 100, 256), dtype=jnp.float32)
        student = jax.random.normal(k2, (16, 150, 256), dtype=jnp.float32)
        return {'teacher_features': teacher, 'student_features': student}
    _L0_xattn_all = _L0_xattn_setup()
    _L0_xattn_in = {k: v for k, v in _L0_xattn_all.items() if k in ()}
    del _L0_xattn_all

    def _L0_ffn_setup():
        import jax, jax.numpy as jnp
        import numpy as np
        B, S, H = (2, 256, 256)
        KD, NH, K = (128, 8, 8)
        NE = 16384
        NK = 64
        EPS = 1e-05
        key = jax.random.key(seed)
        ks = jax.random.split(key, 5)
        inputs = jax.random.normal(ks[0], (B, S, H), jnp.float32)
        bn_gamma = jnp.ones((H,), jnp.float32)
        bn_beta = jnp.zeros((H,), jnp.float32)
        w_q = jax.random.normal(ks[1], (2 * NH * KD, H), jnp.float32) * (1.0 / np.sqrt(H))
        keys_p = jax.random.normal(ks[2], (NH, NK, 2, KD), jnp.float32) * 0.02
        lim = float(np.sqrt(6.0 / (NE + H)))
        down = jax.random.uniform(ks[3], (NE, H), jnp.float32, -lim, lim)
        up = jax.random.uniform(ks[4], (NE, H), jnp.float32, -lim, lim)
        return {'inputs': inputs, 'bn_gamma': bn_gamma, 'bn_beta': bn_beta, 'w_q': w_q, 'keys_p': keys_p, 'down': down, 'up': up}
    _L0_ffn_all = _L0_ffn_setup()
    _L0_ffn_in = {k: v for k, v in _L0_ffn_all.items() if k in ('bn_gamma', 'bn_beta', 'w_q', 'keys_p', 'down', 'up')}
    del _L0_ffn_all
    return {'x': x, 'ctx_1024': ctx_1024, 'L0_attn_qkv_w': _L0_attn_in['qkv_w'], 'L0_attn_qkv_b': _L0_attn_in['qkv_b'], 'L0_attn_proj_w': _L0_attn_in['proj_w'], 'L0_attn_proj_b': _L0_attn_in['proj_b'], 'L0_ffn_bn_gamma': _L0_ffn_in['bn_gamma'], 'L0_ffn_bn_beta': _L0_ffn_in['bn_beta'], 'L0_ffn_w_q': _L0_ffn_in['w_q'], 'L0_ffn_keys_p': _L0_ffn_in['keys_p'], 'L0_ffn_down': _L0_ffn_in['down'], 'L0_ffn_up': _L0_ffn_in['up']}

def reference(x, ctx_1024, L0_attn_qkv_w, L0_attn_qkv_b, L0_attn_proj_w, L0_attn_proj_b, L0_ffn_bn_gamma, L0_ffn_bn_beta, L0_ffn_w_q, L0_ffn_keys_p, L0_ffn_down, L0_ffn_up):
    import jax
    import jax.numpy as jnp

    def _L0_attn_ref(ids, qkv_w, qkv_b, proj_w, proj_b):
        import jax, jax.numpy as jnp
        import numpy as np
        N_HEAD = 16
        B, T, C = ids.shape
        hs = qkv_w.shape[0] // 3
        qkv = ids @ qkv_w.T + qkv_b
        q, k, v = jnp.split(qkv, 3, axis=-1)
        wei = jnp.einsum('btd,bsd->bts', q, k)
        tril = jnp.tril(jnp.ones((T, T), dtype=bool))
        wei = jnp.where(tril, wei, jnp.float32(0.0))
        out_h = jnp.einsum('bts,bsd->btd', wei, v)
        out = jnp.tile(out_h, (1, 1, N_HEAD))
        return out @ proj_w.T + proj_b

    def _L0_xattn_ref(teacher_features, student_features):
        import jax, jax.numpy as jnp
        import numpy as np
        from jax import lax
        BIG = jnp.float32(1e+30)

        def _pairwise_euclidean(a, b):
            aa = jnp.sum(a * a, axis=-1)[:, None]
            bb = jnp.sum(b * b, axis=-1)[None, :]
            ab = a @ b.T
            return jnp.sqrt(jnp.maximum(aa + bb - 2.0 * ab, 0.0))

        def _dtw_cost(D):
            row0 = jnp.cumsum(D[0])

            def row_step(prev_row, d_row):
                first = d_row[0] + prev_row[0]

                def col_step(left, inp):
                    d_ij, up, diag = inp
                    r = d_ij + jnp.minimum(jnp.minimum(up, left), diag)
                    return (r, r)
                _, rest = lax.scan(col_step, first, (d_row[1:], prev_row[1:], prev_row[:-1]))
                row = jnp.concatenate([first[None], rest])
                return (row, row)
            _, rows = lax.scan(row_step, row0, D[1:])
            return jnp.concatenate([row0[None], rows], axis=0)

        def _backtrack(R, T1, T2):
            L = T1 + T2 - 1

            def step(carry, _):
                i, j, done = carry
                valid = jnp.logical_not(done)
                cd = jnp.where((i > 0) & (j > 0), R[jnp.maximum(i - 1, 0), jnp.maximum(j - 1, 0)], BIG)
                cu = jnp.where(i > 0, R[jnp.maximum(i - 1, 0), j], BIG)
                cl = jnp.where(j > 0, R[i, jnp.maximum(j - 1, 0)], BIG)
                choice = jnp.argmin(jnp.stack([cd, cu, cl]))
                ni = jnp.where(choice <= 1, i - 1, i)
                nj = jnp.where((choice == 0) | (choice == 2), j - 1, j)
                at_origin = (i == 0) & (j == 0)
                ni = jnp.where(at_origin, 0, ni)
                nj = jnp.where(at_origin, 0, nj)
                return ((ni, nj, done | at_origin), (i, j, valid))
            init = (jnp.int32(T1 - 1), jnp.int32(T2 - 1), jnp.bool_(False))
            _, (i_idx, j_idx, valid) = lax.scan(step, init, None, length=L)
            return (i_idx, j_idx, valid)

        def _align_one(small, large):
            T_small, d = small.shape
            T_large = large.shape[0]
            D = _pairwise_euclidean(small, large)
            R = _dtw_cost(D)
            i_idx, j_idx, valid = _backtrack(R, T_small, T_large)
            contrib = small[i_idx] * valid[:, None].astype(small.dtype)
            expanded = jnp.zeros((T_large, d), dtype=small.dtype).at[j_idx].add(contrib)
            return expanded
        return jax.vmap(_align_one)(teacher_features, student_features)

    def _L0_ffn_ref(inputs, bn_gamma, bn_beta, w_q, keys_p, down, up):
        import jax, jax.numpy as jnp
        import numpy as np
        B, S, H = (2, 256, 256)
        KD, NH, K = (128, 8, 8)
        NE = 16384
        NK = 64
        EPS = 1e-05
        b, s, d = inputs.shape
        x = inputs.reshape(b * s, d)
        mean = x.mean(axis=0)
        var = x.var(axis=0)
        xn = (x - mean) * jax.lax.rsqrt(var + EPS) * bn_gamma + bn_beta
        xn = xn.reshape(b, s, d)
        q = (xn @ w_q.T).reshape(b, s, 2, NH, KD).transpose(2, 0, 1, 3, 4)
        sim = jnp.einsum('pbnhd,hkpd->pbnhk', q, keys_p)
        scores, idx = jax.lax.top_k(sim, K)
        all_scores = (scores[0][..., :, None] + scores[1][..., None, :]).reshape(b, s, NH, K * K)
        all_idx = (idx[0][..., :, None] * NK + idx[1][..., None, :]).reshape(b, s, NH, K * K)
        sc, pk = jax.lax.top_k(all_scores, K)
        indices = jnp.take_along_axis(all_idx, pk, axis=-1)
        wd = down[indices]
        hmid = jnp.einsum('bnd,bnhkd->bnhk', inputs, wd)
        hmid = jax.nn.sigmoid(sc) * jax.nn.gelu(hmid, approximate=False)
        wu = up[indices]
        return jnp.einsum('bnhk,bnhkd->bnd', hmid, wu)
    x = _layernorm(x + _L0_attn_ref(x, L0_attn_qkv_w, L0_attn_qkv_b, L0_attn_proj_w, L0_attn_proj_b), axis=-1)
    x = _layernorm(x + _L0_xattn_ref(ctx_1024, x), axis=-1)
    x = _layernorm(x + _L0_ffn_ref(x, L0_ffn_bn_gamma, L0_ffn_bn_beta, L0_ffn_w_q, L0_ffn_keys_p, L0_ffn_down, L0_ffn_up), axis=-1)
    return x

_drawn_inputs = setup_inputs


def setup_inputs(seed=0):
    import zlib

    import numpy as np

    out = dict(_drawn_inputs(seed))
    spreads = {'L0_ffn_bn_gamma': (1.0, 0.6), 'L0_ffn_bn_beta': (0.0, 0.8)}
    factors = {'L0_attn_proj_b': 8.0,
     'L0_ffn_w_q': 8.0,
     'L0_ffn_keys_p': 8.0,
     'L0_ffn_down': 8.0,
     'L0_ffn_up': 8.0}
    for name, (base, spread) in spreads.items():
        noise = np.random.default_rng([zlib.crc32(name.encode()), seed]).standard_normal(out[name].shape)
        drawn = base * np.exp(spread * noise) if base else spread * noise
        out[name] = jnp.asarray(drawn.astype(out[name].dtype))
    for name, factor in factors.items():
        out[name] = (out[name] * factor).astype(out[name].dtype)
    return out
```

```python
from contextlib import ExitStack

import concourse.bass as bass
from concourse import mybir

F32 = mybir.dt.float32
I32 = mybir.dt.int32
U32 = mybir.dt.uint32
ALU = mybir.AluOpType
ACT = mybir.ActivationFunctionType
AX = mybir.AxisListType

P = 128
BIG = 1e30
TINY = 1e-30
EPS = 1e-5
ROUND = 8388608.0


def decoder_layer(nc, x, xT, ctx_rows_d, ctx_cols_d, wqkvT_d, bqkv_d, projT_d, projb_d, gamma_d, beta_d, wq_d,
                  keysT_d, table_d, out_d):
    NB, S2, C = ctx_rows_d.shape
    T = x.shape[0] // NB
    NT = T // P
    CC = C // P
    HS = wqkvT_d.shape[1] // 3
    NHEAD = C // HS
    TILES = x.shape[0] // P
    KD, NPH, NK = keysT_d.shape
    NH = NPH // 2
    K = 8
    NE, W2 = table_d.shape
    NG = 4
    RG = (S2 + NG - 1) // NG
    RP = NG * RG
    W = T + 1
    SLOTS = 4
    assert NB == P // NG and C == T == 2 * P and W2 == 2 * C and NK == 64 and KD == P and NH == 2 * SLOTS

    ctx = ExitStack()
    with ctx:
        def sb(name, shape, dt=F32):
            return ctx.enter_context(nc.sbuf_tensor(name, shape, dt))

        def sem(name):
            return ctx.enter_context(nc.semaphore(name))

        x1_d = nc.dram_tensor("x1_scratch", (x.shape[0], C), F32, kind="Internal").ap()
        x2_d = nc.dram_tensor("x2_scratch", (x.shape[0], C), F32, kind="Internal").ap()
        dist_d = nc.dram_tensor("dist_scratch", (NB, RP * T), F32, kind="Internal").ap()

        bank = [ctx.enter_context(nc.psum_tensor(f"bank{i}", [P, 512], F32)) for i in range(8)]

        ident = sb("ident", [P, P])
        iota_i = sb("iota_i", [P, T], I32)
        iota = sb("iota", [P, T])
        iota8 = sb("iota8", [P, K])
        causal = sb("causal", [P, NT, P])
        ones = sb("ones", [P, RP])
        fold = sb("fold", [P, NB])
        wqk = sb("wqk", [P, CC, 48])
        wv = sb("wv", [P, CC, HS])
        bias_qk = sb("bias_qk", [48, 1])
        bias_v = sb("bias_v", [P, HS])
        projT = sb("projT", [HS, C * NHEAD])
        proj = sb("proj", [HS + 1, C])
        gamma = sb("gamma", [P, CC])
        beta = sb("beta", [P, CC])
        keymap = sb("keymap", [P, CC, NPH * NK])
        ctx_rows = sb("ctx_rows", [RP, NB, C])
        ctx_norm = sb("ctx_norm", [RP, NB])
        bn = sb("bn", [P, CC, NB, 6])
        bn_mv = sb("bn_mv", [P, CC, 2])
        bn_scale = sb("bn_scale", [P, CC])
        bn_shift = sb("bn_shift", [P, CC])
        bn_tmp = sb("bn_tmp", [P, CC])
        eps_col = sb("eps_col", [P, 1])

        w_in = sem("w_in")
        wq_in = sem("wq_in")
        ctx_in = sem("ctx_in")
        consts = sem("consts")
        setup_v = sem("setup_v")
        keymap_mm = sem("keymap_mm")
        keymap_done = sem("keymap_done")
        ctx_ready = sem("ctx_ready")
        x_in = [sem(f"x_in{i}") for i in range(2)]
        xT_in = [sem(f"xT_in{i}") for i in range(2)]
        qkv_mm = sem("qkv_mm")
        qk_ready = sem("qk_ready")
        v_ready = sem("v_ready")
        wei_mm = sem("wei_mm")
        weid_ready = sem("weid_ready")
        weio_ready = sem("weio_ready")
        head_mm = sem("head_mm")
        head_ready = sem("head_ready")
        attn_mm = sem("attn_mm")
        sum_done = sem("sum_done")
        var_ready = sem("var_ready")
        std_ready = sem("std_ready")
        x1_ready = sem("x1_ready")
        x1_out = [sem(f"x1_out{i}") for i in range(2)]
        x1T_mm = sem("x1T_mm")
        x1T_ready = sem("x1T_ready")
        ctxm2_ready = sem("ctxm2_ready")
        sq_ready = sem("sq_ready")
        dist_mm = sem("dist_mm")
        dist_ready = sem("dist_ready")
        dist_out = [sem(f"dist_out{i}") for i in range(2)]
        cost_in = [sem(f"cost_in{g}") for g in range(NG)]
        cost_ready = sem("cost_ready")
        table_init = sem("table_init")
        path_init = sem("path_init")
        path_done = sem("path_done")
        bounds_mm = sem("bounds_mm")
        bounds_ready = sem("bounds_ready")
        x1_in = [sem(f"x1_in{i}") for i in range(2)]
        mask_ready = sem("mask_ready")
        warp_mm = sem("warp_mm")
        sum2_done = sem("sum2_done")
        var2_ready = sem("var2_ready")
        std2_ready = sem("std2_ready")
        x2_ready = sem("x2_ready")
        x2_out = [sem(f"x2_out{i}") for i in range(2)]
        x2T_mm = sem("x2T_mm")
        bn_done = sem("bn_done")
        bnvar_ready = sem("bnvar_ready")
        bnstd_ready = sem("bnstd_ready")
        norm_ready = sem("norm_ready")
        pool_rests, dve_rests, act_rests = sem("pool_rests"), sem("dve_rests"), sem("act_rests")
        x2_in = [sem(f"x2_in{i}") for i in range(2)]
        x2c_ready = sem("x2c_ready")
        xT_mm = sem("xT_mm")
        xn_ready = sem("xn_ready")
        score_mm = sem("score_mm")
        scores_read = sem("scores_read")
        idx_ready = sem("idx_ready")
        gate_ready = sem("gate_ready")
        gathered = [sem(f"gathered{i}") for i in range(SLOTS)]
        hid_ready = sem("hid_ready")
        gelu_ready = sem("gelu_ready")
        coef_ready = sem("coef_ready")
        diag_ready = sem("diag_ready")
        chunk_done = sem("chunk_done")
        sum3_done = sem("sum3_done")
        var3_ready = sem("var3_ready")
        std3_ready = sem("std3_ready")
        y_ready = sem("y_ready")
        y_out = [sem(f"y_out{i}") for i in range(2)]

        def rest(eng, spare):
            eng.sem_inc(spare, 1)

        def two_at_a_time(eng, step, first, last, peel):
            for b in range(first, first + peel):
                step(b, b // 2, b % 2)
            lo = first + peel
            pairs = (last - lo) // 2
            if pairs:
                with eng.Fori(lo // 2, lo // 2 + pairs) as j:
                    for par in range(2):
                        step(2 * j + par, j, par)
            for b in range(lo + 2 * pairs, last):
                step(b, b // 2, b % 2)

        with ExitStack() as st:
            def sa(name, shape, dt=F32):
                return st.enter_context(nc.sbuf_tensor(name, shape, dt))

            wq_rows = sa("wq_rows", [P, NPH, C])
            keysT = sa("keysT", [P, NPH, NK])
            ctx_cols = sa("ctx_cols", [P, CC, NB, S2])
            ctxm2 = sa("ctxm2", [P, 2, CC, RP])
            x_sb = sa("x_sb", [P, 2, NT, C])
            xT_sb = sa("xT_sb", [P, 2, CC, T])
            qT = sa("qT", [HS, T])
            kT = sa("kT", [HS, T])
            v_sb = sa("v_sb", [P, 2, NT, HS])
            weiT = sa("weiT", [P, 3, P])
            headT = sa("headT", [HS + 1, T])
            y1 = sa("y1", [P, NT, C])
            st1 = sa("st1", [P, NT, 6])
            mv1 = sa("mv1", [P, NT, 2])
            sd1 = sa("sd1", [P, NT])
            rs1 = sa("rs1", [P, NT])
            x1_sb = sa("x1_sb", [P, 2, NT, C])
            x1T = sa("x1T", [P, CC, T])
            x1sq = sa("x1sq", [P, CC, T])
            x1sum = sa("x1sum", [P, T])
            dist_sb = sa("dist_sb", [RP, 2, T])
            sq_scr = sa("sq_scr", [RP, 8, C])

            ps_qk, ps_v = bank[0][0:48, 0:T], bank[6][:, 0:NT * HS].rearrange("p (t d) -> p t d", t=NT)
            ps_wei = bank[1][:, 0:3 * P].rearrange("p (k t) -> p k t", k=3)
            ps_head = bank[2][0:HS, 0:T]
            ps_attn = bank[3][:, :].rearrange("p (t c) -> p t c", t=NT)
            ps_x1T = bank[4][:, :].rearrange("p (c t) -> p c t", c=CC)
            ps_dist = bank[5][0:RP, 0:T]
            ps_key = [bank[i] for i in range(4)]

            block = st.enter_context(nc.Block())
            xb = x.rearrange("(b t p) c -> b p t c", b=NB, t=NT)
            x1b = x1_d.rearrange("(b t p) c -> b p t c", b=NB, t=NT)
            xTb = xT.rearrange("(k p) (b t) -> b p k t", k=CC, b=NB)
            LAG = 2

            @block.sync
            def _(sp):
                def load_xT(b, h, par):
                    if not (isinstance(b, int) and b < 2):
                        sp.wait_ge(qkv_mm, b - 1)
                    sp.dma_start(xT_sb[:, par], flat(xTb, b)).then_inc(xT_in[par], 16)

                def load_x(b, h, par):
                    if not (isinstance(b, int) and b < 2):
                        sp.wait_ge(sum_done, b - 1)
                    sp.dma_start(x_sb[:, par], flat(xb, b)).then_inc(x_in[par], 16)

                def store_x1(b, h, par):
                    sp.wait_ge(x1_ready, b + 1)
                    sp.dma_start(flat(x1b, b), x1_sb[:, par]).then_inc(x1_out[par], 16)

                def store_dist(b, h, par):
                    sp.wait_ge(dist_ready, b + 1)
                    sp.dma_start(dist_d[ds1(b)].rearrange("a (i j) -> (a i) j", i=RP),
                                 dist_sb[:, par]).then_inc(dist_out[par], 16)

                def flat(ap, b):
                    return ap[ds1(b)].rearrange("a p t c -> (a p) t c")

                def ds1(b):
                    return bass.ds(b, 1)

                for dst, src in ((wqk[:, :, 0:HS], wqkvT_d[:, 0:HS].rearrange("(k p) d -> p k d", k=CC)),
                                 (wqk[:, :, 32:32 + HS], wqkvT_d[:, HS:2 * HS].rearrange("(k p) d -> p k d", k=CC)),
                                 (wv[:, :, :], wqkvT_d[:, 2 * HS:].rearrange("(k p) d -> p k d", k=CC)),
                                 (bias_qk[0:HS, :], bqkv_d[0:HS]), (bias_qk[32:32 + HS, :], bqkv_d[HS:2 * HS]),
                                 (bias_v[:, :], bqkv_d[2 * HS:].rearrange("d a -> a d").partition_broadcast(P)
                                  if False else bqkv_d[2 * HS:].rearrange("d a -> a d").to_broadcast([P, HS])),
                                 (projT[:, :], projT_d), (proj[HS:HS + 1, :], projb_d),
                                 (gamma[:, :], gamma_d), (beta[:, :], beta_d)):
                    sp.dma_start(dst, src).then_inc(w_in, 16)
                for b in range(2):
                    load_xT(b, 0, b)
                    load_x(b, 0, b)
                sp.dma_start(ctx_cols[:, :, :, :], ctx_cols_d.rearrange("(k p) b s -> p k b s", k=CC))\
                    .then_inc(ctx_in, 16)
                sp.wait_ge(consts, 6)
                sp.dma_start(ctx_rows[0:S2, :, :], ctx_rows_d.rearrange("b s c -> s b c")).then_inc(ctx_in, 16)
                sp.dma_start(keysT[:, :, :], keysT_d).then_inc(wq_in, 16)
                sp.dma_start(wq_rows[:, :, :], wq_d.rearrange("(g d) c -> d g c", g=NPH)).then_inc(wq_in, 16)

                def step(i, h, par):
                    load_xT(i, h, par)
                    store_x1(i - 2, h, par)
                    load_x(i, h, par)
                    if not (isinstance(i, int) and i < 3):
                        store_dist(i - 3, h, 1 - par)
                two_at_a_time(sp, step, 2, NB, 2)
                for b in range(NB - 2, NB):
                    store_x1(b, b // 2, b % 2)
                    store_dist(b - 1, b // 2, 1 - b % 2)
                store_dist(NB - 1, 0, 1)
                for par in range(2):
                    sp.wait_ge(x1_out[par], 16 * NB // 2)
                    sp.wait_ge(dist_out[par], 16 * NB // 2)

            @block.gpsimd
            def _(pool):
                pool.memset(ident[:, :], 0.0)
                pool.memset(causal[:, :, :], 1.0)
                pool.memset(ones[:, :], 1.0)
                pool.memset(ctxm2[:, :, :, :], 0.0)
                pool.memset(headT[:, :], 1.0)
                pool.drain()
                pool.memset(ctx_rows[64:RP, :, :], 0.0)
                pool.drain()
                pool.memset(wqk[:, :, HS:32], 0.0)
                pool.memset(eps_col[:, :], EPS)
                pool.iota(iota_i[:, :], [[1, T]], base=0, channel_multiplier=0)
                pool.drain()
                pool.affine_select(out=ident[:, :], in_=ident[:, :], compare_op=ALU.not_equal, fill=1.0, base=0,
                                   pattern=[[-1, P]], channel_multiplier=1)
                pool.affine_select(out=causal[:, :, :], in_=causal[:, :, :], compare_op=ALU.is_ge, fill=0.0,
                                   base=0, pattern=[[0, NT], [1, P]], channel_multiplier=-1)
                pool.drain()
                pool.nop().then_inc(consts, 6)

                def squares(b, h, par):
                    pool.wait_ge(x1T_ready, b + 1)
                    pool.tensor_tensor(x1sq[:, :, :], x1T[:, :, :], x1T[:, :, :], ALU.mult)
                    pool.drain()
                    if not (isinstance(b, int) and b < 1):
                        pool.wait_ge(dist_mm, b)
                    pool.tensor_tensor(x1sum[:, :], x1sq[:, 0, :], x1sq[:, 1, :], ALU.add).then_inc(sq_ready, 1)
                two_at_a_time(pool, squares, 0, NB, 2)

            @block.tensor
            def _(pe):
                def qkv(b, h, par):
                    pe.wait_ge(xT_in[par], 16 * h + 16)
                    if not (isinstance(b, int) and b < 1):
                        pe.wait_ge(qk_ready, b)
                        pe.wait_ge(v_ready, b)
                    for c in range(CC):
                        pe.matmul(ps_qk, wqk[:, c, :], xT_sb[:, par, c, :], start=(c == 0), stop=(c == CC - 1))
                    for t in range(NT):
                        for c in range(CC):
                            mm = pe.matmul(ps_v[:, t, :], xT_sb[:, par, c, t * P:(t + 1) * P], wv[:, c, :],
                                           start=(c == 0), stop=(c == CC - 1))
                    mm.then_inc(qkv_mm, 1)

                def wei(b, h, par):
                    pe.wait_ge(qk_ready, b + 1)
                    if not (isinstance(b, int) and b < 1):
                        pe.wait_ge(weid_ready, b)
                        pe.wait_ge(weio_ready, b)
                    pe.matmul(ps_wei[:, 0, :], kT[:, P:T], qT[:, P:T], start=True, stop=True)
                    pe.matmul(ps_wei[:, 1:3, :].rearrange("p k t -> p (k t)"), kT[:, 0:P], qT[:, :],
                              start=True, stop=True).then_inc(wei_mm, 1)

                def head(b, h, par):
                    pe.wait_ge(v_ready, b + 1)
                    pe.wait_ge(weid_ready, b + 1)
                    pe.wait_ge(weio_ready, b + 1)
                    if not (isinstance(b, int) and b < 1):
                        pe.wait_ge(head_ready, b)
                    pe.matmul(ps_head, v_sb[:, par, 0, :], weiT[:, 1:3, :].rearrange("p k t -> p (k t)"),
                              start=True, stop=False)
                    pe.matmul(ps_head[:, P:T], v_sb[:, par, 1, :], weiT[:, 0, :], start=False, stop=True)\
                        .then_inc(head_mm, 1)

                def attn(b, h, par):
                    pe.wait_ge(head_ready, b + 1)
                    if not (isinstance(b, int) and b < 1):
                        pe.wait_ge(sum_done, b)
                    for t in range(NT):
                        mm = pe.matmul(ps_attn[:, t, :], headT[:, t * P:(t + 1) * P], proj[:, :],
                                       start=True, stop=True)
                    mm.then_inc(attn_mm, 1)

                def turn_x1(b, h, par):
                    pe.wait_ge(x1_ready, b + 1)
                    if not (isinstance(b, int) and b < 1):
                        pe.wait_ge(x1T_ready, b)
                    for c in range(CC):
                        for t in range(NT):
                            mm = pe.transpose(ps_x1T[:, c, t * P:(t + 1) * P], x1_sb[:, par, t, c * P:(c + 1) * P],
                                              ident[:, :])
                    mm.then_inc(x1T_mm, 1)

                def dist(b, h, par):
                    pe.wait_ge(ctxm2_ready, b + 1)
                    pe.wait_ge(x1T_ready, b + 1)
                    if not (isinstance(b, int) and b < 1):
                        pe.wait_ge(dist_ready, b)
                    for c in range(CC):
                        pe.matmul(ps_dist, ctxm2[:, par, c, :], x1T[:, c, :], start=(c == 0), stop=False)
                    pe.wait_ge(sq_ready, b + 1)
                    pe.matmul(ps_dist, ones[:, :], x1sum[:, :], start=False, stop=True).then_inc(dist_mm, 1)

                pe.wait_ge(consts, 6)
                pe.wait_ge(wq_in, 32)
                for c in range(CC):
                    for g in range(NPH):
                        mm = pe.matmul(ps_key[2 * c + g // NH][:, (g % NH) * NK:(g % NH + 1) * NK],
                                       wq_rows[:, g, c * P:(c + 1) * P], keysT[:, g, :], start=True, stop=True)
                mm.then_inc(keymap_mm, 1)
                pe.wait_ge(keymap_done, 1)
                pe.wait_ge(w_in, 16 * 10)
                pe.wait_ge(setup_v, 1)

                def step(i, h, par):
                    a = (i, h, par)
                    b = (i - 1, None, 1 - par)
                    c = (i - 2, None, par)
                    n = i if isinstance(i, int) else None
                    if n is None or n < NB:
                        qkv(*a)
                    if n is None or 1 <= n <= NB:
                        wei(*b)
                    if n is None or n >= 2:
                        turn_x1(*c)
                    if n is None or 1 <= n <= NB:
                        head(*b)
                    if n is None or n >= 2:
                        dist(*c)
                    if n is None or 1 <= n <= NB:
                        attn(*b)
                for n in range(4):
                    step(n, n // 2, n % 2)
                two_at_a_time(pe, step, 4, NB, 0)
                for n in range(NB, NB + 2):
                    step(n, n // 2, n % 2)

            @block.scalar
            def _(act):
                def qk(b, h, par):
                    act.wait_ge(qkv_mm, b + 1)
                    if not (isinstance(b, int) and b < 1):
                        act.wait_ge(wei_mm, b)
                    act.activation(qT[:, :], ps_qk[0:HS, :], ACT.Identity, bias=bias_qk[0:HS, :])
                    act.activation(kT[:, :], ps_qk[32:32 + HS, :], ACT.Identity, bias=bias_qk[32:32 + HS, :])\
                        .then_inc(qk_ready, 1)

                def wei_off(b, h, par):
                    act.wait_ge(weid_ready, b + 1)
                    act.wait_ge(wei_mm, b + 1)
                    if not (isinstance(b, int) and b < 1):
                        act.wait_ge(head_mm, b)
                    act.activation(weiT[:, 2, :], ps_wei[:, 2, :], ACT.Copy).then_inc(weio_ready, 1)

                def x1_cols(b, h, par):
                    act.wait_ge(x1T_mm, b + 1)
                    if not (isinstance(b, int) and b < 1):
                        act.wait_ge(dist_mm, b)
                        act.wait_ge(sq_ready, b)
                    act.activation(x1T[:, :, :], ps_x1T[:, :, :], ACT.Copy).then_inc(x1T_ready, 1)

                def ctx_scale(b, h, par):
                    if not (isinstance(b, int) and b < 2):
                        act.wait_ge(dist_mm, b - 1)
                    rest(act, act_rests)
                    act.activation(ctxm2[:, par, :, 0:S2],
                                   ctx_cols[:, :, bass.ds(b, 1), :].rearrange("p k a s -> p k (a s)"),
                                   ACT.Copy, scale=-2.0).then_inc(ctxm2_ready, 1)

                def head(b, h, par):
                    act.wait_ge(head_mm, b + 1)
                    if not (isinstance(b, int) and b < 1):
                        act.wait_ge(attn_mm, b)
                    act.activation(headT[0:HS, :], ps_head, ACT.Copy).then_inc(head_ready, 1)

                def std(b, h, par):
                    act.wait_ge(var_ready, b + 1)
                    act.activation(sd1[:, :], mv1[:, :, 1], ACT.Sqrt, bias=eps_col[:, :]).then_inc(std_ready, 1)

                act.wait_ge(consts, 6)
                act.wait_ge(w_in, 160)
                act.wait_ge(keymap_mm, 1)
                for i in range(4):
                    kc = act.activation(keymap[:, i // 2, (i % 2) * 512:(i % 2 + 1) * 512], ps_key[i][:, :], ACT.Copy)
                kc.then_inc(keymap_done, 1)
                act.wait_ge(ctx_in, 32)

                def step(i, h, par):
                    a = (i, h, par)
                    b = (i - 1, None, 1 - par)
                    c = (i - 2, None, par)
                    n = i if isinstance(i, int) else None
                    if n is None or n < NB:
                        qk(*a)
                    if n is None or 1 <= n <= NB:
                        wei_off(*b)
                    if n is None or n >= 2:
                        ctx_scale(*c)
                        x1_cols(*c)
                    if n is None or 1 <= n <= NB:
                        head(*b)
                        std(*b)
                for n in range(4):
                    step(n, n // 2, n % 2)
                two_at_a_time(act, step, 4, NB, 0)
                for n in range(NB, NB + 2):
                    step(n, n // 2, n % 2)

            @block.vector
            def _(dve):
                def v(b, h, par):
                    dve.wait_ge(qkv_mm, b + 1)
                    if not (isinstance(b, int) and b < 2):
                        dve.wait_ge(head_mm, b - 1)
                    dve.tensor_tensor(v_sb[:, par], ps_v, bias_v[:, None, :].to_broadcast([P, NT, HS]), ALU.add)\
                        .then_inc(v_ready, 1)

                def wei_diag(b, h, par):
                    dve.wait_ge(wei_mm, b + 1)
                    if not (isinstance(b, int) and b < 1):
                        dve.wait_ge(head_mm, b)
                    dve.tensor_tensor(weiT[:, 0:2, :], ps_wei[:, 0:2, :], causal[:, :, :], ALU.mult)\
                        .then_inc(weid_ready, 1)

                def dist(b, h, par):
                    dve.wait_ge(dist_mm, b + 1)
                    if not (isinstance(b, int) and b < 2):
                        dve.wait_ge(dist_out[par], dma_count(b, par) - 16)
                    dve.tensor_scalar(dist_sb[:, par, :], ps_dist, ctx_norm[:, bass.ds(b, 1)], TINY, ALU.add, ALU.max)\
                        .then_inc(dist_ready, 1)

                def dma_count(b, par):
                    return 8 * (b - par) + 16

                def norm(b, h, par):
                    dve.wait_ge(attn_mm, b + 1)
                    dve.wait_ge(x_in[par], dma_count(b, par))
                    dve.tensor_tensor(y1[:, :, :], ps_attn, x_sb[:, par], ALU.add).then_inc(sum_done, 1)
                    dve.drain()
                    for t in range(NT):
                        dve.bn_stats(out=st1[:, t, :], in_=y1[:, t, :])
                    dve.drain()
                    for t in range(NT):
                        last = dve.bn_aggr(out=mv1[:, t, :], in_=st1[:, t, :])
                    last.then_inc(var_ready, 1)

                def scale(b, h, par):
                    dve.wait_ge(std_ready, b + 1)
                    dve.reciprocal(rs1[:, :], sd1[:, :])
                    dve.drain()
                    if not (isinstance(b, int) and b < 2):
                        dve.wait_ge(x1_out[par], dma_count(b, par) - 16)
                        dve.wait_ge(x1T_mm, b - 1)
                    for t in range(NT):
                        last = dve.tensor_scalar(x1_sb[:, par, t, :], y1[:, t, :], mv1[:, t, 0:1], rs1[:, t:t + 1],
                                                 ALU.subtract, ALU.mult)
                    last.then_inc(x1_ready, 1)

                dve.wait_ge(consts, 6)
                dve.wait_ge(w_in, 160)
                dve.tensor_copy(iota[:, :], iota_i[:, :])
                dve.tensor_copy(iota8[:, :], iota_i[:, 0:K])
                dve.tensor_reduce(fold[:, :], ident[:, :].rearrange("p (g b) -> p b g", g=NG), AX.X, ALU.add)
                dve.tensor_reduce(proj[0:HS, :], projT[:, :].rearrange("d (c h) -> d c h", h=NHEAD), AX.X, ALU.add)\
                    .then_inc(setup_v, 1)
                dve.wait_ge(ctx_in, 32)
                for b in range(NB):
                    if b % 8 == 0:
                        dve.drain()
                    dve.tensor_tensor_reduce(out=sq_scr[:, b % 8, :], in0=ctx_rows[:, b, :], in1=ctx_rows[:, b, :], scale=1.0,
                                             scalar=0.0, op0=ALU.mult, op1=ALU.add, accum_out=ctx_norm[:, b:b + 1])
                dve.drain()

                def step(i, h, par):
                    a = (i, h, par)
                    b = (i - 1, None, 1 - par)
                    c = (i - 2, None, par)
                    n = i if isinstance(i, int) else None
                    if n is None or n < NB:
                        v(*a)
                    if n is None or 1 <= n <= NB:
                        wei_diag(*b)
                    if n is None or n >= 2:
                        dist(*c)
                    if n is None or 1 <= n <= NB:
                        norm(*b)
                        scale(*b)
                for n in range(4):
                    step(n, n // 2, n % 2)
                two_at_a_time(dve, step, 4, NB, 0)
                for n in range(NB, NB + 2):
                    step(n, n // 2, n % 2)

        with ExitStack() as st:
            def sw(name, shape, dt=F32):
                return st.enter_context(nc.sbuf_tensor(name, shape, dt))

            cost = sw("cost", [P, RG * T])
            acc = sw("acc", [P, (RG + 1) * W])
            best = sw("best", [P, RG * T])
            is_left = sw("is_left", [P, RG * T])
            entry = sw("entry", [P, RG * T])
            pick = sw("pick", [P, T])
            lo_hi = sw("lo_hi", [P, 2, RP])
            bounds = sw("bounds", [RP, 2, NB])
            above = sw("above", [S2, 2, T])
            mask = sw("mask", [S2, 2, T])
            x1_sb = sw("x1_again", [P, 2, NT, C])
            y2 = sw("y2", [P, NT, C])
            st2 = sw("st2", [P, NT, 6])
            mv2 = sw("mv2", [P, NT, 2])
            sd2 = sw("sd2", [P, NT])
            rs2 = sw("rs2", [P, NT])
            x2_sb = sw("x2_sb", [P, 2, NT, C])
            ps_bounds = bank[0][0:RP, 0:2 * NB].rearrange("p (a b) -> p a b", a=2)
            ps_warp = [bank[1 + i][:, :].rearrange("p (t c) -> p t c", t=NT) for i in range(2)]
            ps_x2T = [bank[3 + i][:, :].rearrange("p (c t) -> p c t", c=CC) for i in range(2)]
            x1b = x1_d.rearrange("(b t p) c -> b p t c", b=NB, t=NT)
            x2b = x2_d.rearrange("(b t p) c -> b p t c", b=NB, t=NT)
            acc3 = acc[:, :].rearrange("p (r w) -> p r w", w=W)

            block = st.enter_context(nc.Block())

            @block.sync
            def _(sp):
                for g in range(NG):
                    sp.dma_start(cost[NB * g:NB * (g + 1), :], dist_d[:, RG * T * g:RG * T * (g + 1)])\
                        .then_inc(cost_in[g], 16)

                def one(ap, b):
                    return ap[bass.ds(b, 1)].rearrange("a p t c -> (a p) t c")

                def load(b, h, par):
                    if not (isinstance(b, int) and b < 2):
                        sp.wait_ge(sum2_done, b - 1)
                    sp.dma_start(x1_sb[:, par], one(x1b, b)).then_inc(x1_in[par], 16)

                def store(b, h, par):
                    sp.wait_ge(x2_ready, b + 1)
                    sp.dma_start(one(x2b, b), x2_sb[:, par]).then_inc(x2_out[par], 16)

                load(0, 0, 0)
                load(1, 0, 1)

                def step(i, h, par):
                    store(i - 2, h - 1, par)
                    load(i, h, par)
                two_at_a_time(sp, step, 2, NB, 2)
                for b in range(NB - 2, NB):
                    store(b, b // 2, b % 2)
                for par in range(2):
                    sp.wait_ge(x2_out[par], 16 * NB // 2)

            @block.gpsimd
            def _(pool):
                pool.memset(acc[:, :], BIG)
                pool.drain()
                pool.memset(acc[0:NB, 0:1], 0.0)
                pool.memset(best[:, :], BIG)
                pool.memset(lo_hi[:, :, :], 0.0)
                pool.drain()
                pool.nop().then_inc(table_init, 1)

            @block.scalar
            def _(act):
                for g in range(NG):
                    q = slice(NB * g, NB * (g + 1))
                    act.wait_ge(cost_in[g], 16)
                    act.activation(cost[q, :], cost[q, :], ACT.Sqrt).then_inc(cost_ready, 1)
                act.wait_ge(bounds_mm, 1)
                act.activation(bounds[:, :, :], ps_bounds, ACT.Copy).then_inc(bounds_ready, 1)

                def std(b, h, par):
                    act.wait_ge(var2_ready, b + 1)
                    act.activation(sd2[:, :], mv2[:, :, 1], ACT.Sqrt, bias=eps_col[:, :]).then_inc(std2_ready, 1)
                two_at_a_time(act, std, 0, NB, 0)
                act.wait_ge(bnvar_ready, 1)
                act.activation(bn_tmp[:, :], bn_mv[:, :, 1], ACT.Sqrt, bias=eps_col[:, :]).then_inc(bnstd_ready, 1)

            @block.tensor
            def _(pe):
                pe.wait_ge(path_done, 1)
                for a in range(2):
                    mm = pe.matmul(ps_bounds[:, a, :], lo_hi[:, a, :], fold[:, :], start=True, stop=True)
                mm.then_inc(bounds_mm, 1)

                def warp(b, h, par):
                    pe.wait_ge(mask_ready, b + 1)
                    if not (isinstance(b, int) and b < 2):
                        pe.wait_ge(sum2_done, b - 1)
                    for t in range(NT):
                        mm = pe.matmul(ps_warp[par][:, t, :], mask[:, par, t * P:(t + 1) * P],
                                       ctx_rows[0:S2, bass.ds(b, 1), :].rearrange("s a c -> s (a c)"),
                                       start=True, stop=True)
                    mm.then_inc(warp_mm, 1)

                def turn(b, h, par):
                    pe.wait_ge(x2_ready, b + 1)
                    if not (isinstance(b, int) and b < 2):
                        pe.wait_ge(bn_done, b - 1)
                    for c in range(CC):
                        for t in range(NT):
                            mm = pe.transpose(ps_x2T[par][:, c, t * P:(t + 1) * P],
                                              x2_sb[:, par, t, c * P:(c + 1) * P], ident[:, :])
                    mm.then_inc(x2T_mm, 1)
                warp(0, 0, 0)

                def step(i, h, par):
                    warp(i, h, par)
                    turn(i - 1, None, 1 - par)
                two_at_a_time(pe, step, 1, NB, 3)
                turn(NB - 1, None, 1)

            @block.vector
            def _(dve):
                dve.wait_ge(table_init, 1)
                for g in range(NG):
                    q = slice(NB * g, NB * (g + 1))
                    rows = min(RG, S2 - RG * g)
                    dve.wait_ge(cost_ready, g + 1)
                    if g:
                        dve.tensor_copy(acc[q, 0:W], acc[NB * (g - 1):NB * g, RG * W:(RG + 1) * W])
                        dve.drain()

                    def row(r):
                        dve.tensor_tensor(best[q, bass.ds(r * T, T)], acc[q, bass.ds(r * W + 1, T)],
                                          acc[q, bass.ds(r * W, T)], ALU.min)
                        dve.drain()
                        dve.tensor_tensor_scan(acc[q, bass.ds(r * W + W + 1, T)], best[q, bass.ds(r * T, T)],
                                               cost[q, bass.ds(r * T, T)], BIG, ALU.min, ALU.add)
                        dve.drain()
                    U = 4
                    with dve.Fori(0, rows // U) as i:
                        for u in range(U):
                            row(i * U + u)
                    for r in range(rows // U * U, rows):
                        row(r)

                best3 = best[:, :].rearrange("p (r t) -> p r t", t=T)
                left3 = is_left[:, :].rearrange("p (r t) -> p r t", t=T)
                entry3 = entry[:, :].rearrange("p (r t) -> p r t", t=T)
                dve.tensor_tensor(left3, acc3[:, 1:, 0:T], best3, ALU.is_lt)
                dve.tensor_tensor(entry3, acc3[:, 0:RG, 0:T], acc3[:, 0:RG, 1:W], ALU.is_le)
                dve.drain()
                dve.scalar_tensor_tensor(out=best3, in0=entry3, scalar=-0.75,
                                         in1=iota[:, None, :].to_broadcast([P, RG, T]), op0=ALU.mult, op1=ALU.add)
                dve.drain()
                dve.scalar_tensor_tensor(out=best[:, :], in0=is_left[:, :], scalar=-1.0, in1=best[:, :],
                                         op0=ALU.add, op1=ALU.mult)
                dve.drain()
                dve.tensor_tensor_scan(entry[:, :], is_left[:, :], best[:, :], 0.0, ALU.mult, ALU.subtract)

                last = S2 - 1
                g = last // RG
                dve.memset(lo_hi[NB * g:NB * (g + 1), 1, last:last + 1], float(T - 1))
                dve.drain()

                def climb(i, g, g_next):
                    q, up = slice(NB * g, NB * (g + 1)), slice(NB * g_next, NB * (g_next + 1))
                    dve.scalar_tensor_tensor(out=pick[q, :], in0=iota[q, :], scalar=lo_hi[q, 1, bass.ds(i, 1)],
                                             in1=entry[q, bass.ds((i - RG * g) * T, T)], op0=ALU.is_equal, op1=ALU.mult,
                                             accum_out=lo_hi[q, 0, bass.ds(i, 1)])
                    dve.drain()
                    if g_next is not None:
                        dve.tensor_scalar(lo_hi[up, 1, bass.ds(i - 1, 1)], lo_hi[q, 0, bass.ds(i, 1)], ROUND, ROUND,
                                          ALU.add, ALU.subtract)
                        dve.drain()
                for g in range(NG - 1, -1, -1):
                    top, bottom = RG * g, min(RG * (g + 1), S2) - 1
                    U = 4
                    n = (bottom - top) // U
                    with dve.Fori(0, n) as j:
                        for u in range(U):
                            climb(bottom - u - j * U, g, g)
                    for i in range(bottom - n * U, top, -1):
                        climb(i, g, g)
                    if g:
                        climb(top, g, g - 1)
                dve.scalar_tensor_tensor(out=pick[0:NB, :], in0=iota[0:NB, :], scalar=lo_hi[0:NB, 1, 0:1],
                                         in1=entry[0:NB, 0:T], op0=ALU.is_equal, op1=ALU.mult,
                                         accum_out=lo_hi[0:NB, 0, 0:1])
                dve.drain()
                dve.nop().then_inc(path_done, 1)
                dve.wait_ge(bounds_ready, 1)

                def masks(b, h, par):
                    dve.tensor_scalar(above[:, par, :], iota[0:S2, :], bounds[0:S2, 0, bass.ds(b, 1)], None, ALU.is_ge)
                    dve.drain()
                    if not (isinstance(b, int) and b < 2):
                        dve.wait_ge(warp_mm, b - 1)
                    dve.scalar_tensor_tensor(out=mask[:, par, :], in0=iota[0:S2, :],
                                             scalar=bounds[0:S2, 1, bass.ds(b, 1)], in1=above[:, par, :],
                                             op0=ALU.is_le, op1=ALU.mult).then_inc(mask_ready, 1)

                def norm(b, h, par):
                    dve.wait_ge(warp_mm, b + 1)
                    dve.wait_ge(x1_in[par], 8 * (b - par) + 16)
                    dve.tensor_tensor(y2[:, :, :], ps_warp[par], x1_sb[:, par], ALU.add).then_inc(sum2_done, 1)
                    dve.drain()
                    for t in range(NT):
                        dve.bn_stats(out=st2[:, t, :], in_=y2[:, t, :])
                    dve.drain()
                    for t in range(NT):
                        last = dve.bn_aggr(out=mv2[:, t, :], in_=st2[:, t, :])
                    last.then_inc(var2_ready, 1)

                def scale(b, h, par):
                    dve.wait_ge(std2_ready, b + 1)
                    dve.reciprocal(rs2[:, :], sd2[:, :])
                    dve.drain()
                    if not (isinstance(b, int) and b < 2):
                        dve.wait_ge(x2_out[par], 8 * (b - par))
                        dve.wait_ge(x2T_mm, b - 1)
                    for t in range(NT):
                        last = dve.tensor_scalar(x2_sb[:, par, t, :], y2[:, t, :], mv2[:, t, 0:1], rs2[:, t:t + 1],
                                                 ALU.subtract, ALU.mult)
                    last.then_inc(x2_ready, 1)

                def stats(b, h, par):
                    dve.wait_ge(x2T_mm, b + 1)
                    for c in range(CC):
                        last = dve.bn_stats(out=bn[:, c, bass.ds(b, 1), :].rearrange("p a s -> p (a s)"),
                                            in_=ps_x2T[par][:, c, :])
                    last.then_inc(bn_done, 1)
                masks(0, 0, 0)

                def step(i, h, par):
                    masks(i, h, par)
                    norm(i - 1, None, 1 - par)
                    if not (isinstance(i, int) and i < 2):
                        stats(i - 2, None, par)
                    scale(i - 1, None, 1 - par)
                two_at_a_time(dve, step, 1, NB, 3)
                dve.drain()
                norm(NB - 1, None, 1)
                stats(NB - 2, None, 0)
                scale(NB - 1, None, 1)
                stats(NB - 1, None, 1)
                dve.drain()
                for c in range(CC):
                    last = dve.bn_aggr(out=bn_mv[:, c, :], in_=bn[:, c, :, :].rearrange("p b s -> p (b s)"))
                last.then_inc(bnvar_ready, 1)
                dve.wait_ge(bnstd_ready, 1)
                dve.reciprocal(bn_scale[:, :], bn_tmp[:, :])
                dve.drain()
                dve.tensor_tensor(bn_scale[:, :], bn_scale[:, :], gamma[:, :], ALU.mult)
                dve.drain()
                dve.tensor_tensor(bn_tmp[:, :], bn_mv[:, :, 0], bn_scale[:, :], ALU.mult)
                dve.drain()
                dve.tensor_tensor(bn_shift[:, :], beta[:, :], bn_tmp[:, :], ALU.subtract).then_inc(norm_ready, 1)

        with ExitStack() as st:
            def se(name, shape, dt=F32):
                return st.enter_context(nc.sbuf_tensor(name, shape, dt))

            HK = NH * K
            x2_sb = se("x2_tile", [P, 2, C])
            xnT = se("xnT", [P, CC, P])
            top = se("top", [P, 2, NH, K])
            top_i = se("top_i", [P, 2, NH, K], U32)
            pair = se("pair", [P, NH, K, K])
            sel = se("sel", [P, NH, K])
            sel_i = se("sel_i", [P, NH, K], U32)
            half_i = se("half_i", [P, 2, HK], U32)
            hot = se("hot", [P, 2, HK, K])
            half_key = se("half_key", [P, 2, HK])
            idx = se("idx", [P, 2, HK], U32)
            gate = se("gate", [P, 2, HK])
            rows = se("rows", [P, SLOTS, K, W2])
            hid = se("hid", [P, 2, HK])
            gel = se("gel", [P, 2, HK])
            coef = se("coef", [P, 2, HK])
            diag = se("diag", [P, 2, K, P])
            y3 = se("y3", [P, C])
            st3 = se("st3", [P, 6])
            mv3 = se("mv3", [P, 2])
            sd3 = se("sd3", [P, 1])
            rs3 = se("rs3", [P, 1])
            yo = se("yo", [P, 2, C])
            ps_score = bank[0], bank[1]
            ps_xT = bank[2][:, 0:C].rearrange("p (c t) -> p c t", c=CC)
            ps_x2 = [bank[3][:, 0:C], bank[4][:, 0:C]]
            ps_out = [bank[5][:, 0:C], bank[6][:, 0:C]]
            x2t = x2_d.rearrange("(n p) c -> n p c", p=P)
            outt = out_d.rearrange("(n p) c -> n p c", p=P)
            ROUTE_AT = 3

            def tiles(eng, step):
                for n in range(2):
                    step(n, n)
                with eng.Fori(1, TILES // 2 - 1) as j:
                    for par in range(2):
                        step(2 * j + par, par)
                for n in range(TILES - 2, TILES):
                    step(n, n % 2)

            block = st.enter_context(nc.Block())

            @block.sync
            def _(sp):
                def load(n, par):
                    if not (isinstance(n, int) and n < 2):
                        sp.wait_ge(sum3_done, n - 1)
                        sp.wait_ge(xT_mm, n - 1)
                        sp.wait_ge(x2c_ready, n - 1)
                    sp.dma_start(x2_sb[:, par], x2t[bass.ds(n, 1)].rearrange("a p c -> (a p) c"))\
                        .then_inc(x2_in[par], 16)

                def store(n, par):
                    sp.wait_ge(y_ready, n + 1)
                    sp.dma_start(outt[bass.ds(n, 1)].rearrange("a p c -> (a p) c"), yo[:, par])\
                        .then_inc(y_out[par], 16)
                load(0, 0)

                def step(n, par):
                    if not (isinstance(n, int) and n < 1):
                        pass
                    if not (isinstance(n, int) and n == TILES - 1):
                        load(n + 1, 1 - par)
                    if not (isinstance(n, int) and n < 1):
                        store(n - 1, 1 - par)
                tiles(sp, step)
                store(TILES - 1, 1)
                for par in range(2):
                    sp.wait_ge(y_out[par], 16 * TILES // 2)

            @block.gpsimd
            def _(pool):
                def step(n, par):
                    pool.wait_ge(idx_ready, n + 1)
                    for h in range(NH):
                        if not (isinstance(n, int) and n * NH + h < SLOTS):
                            pool.wait_ge(chunk_done, n * NH + (h + 1 - SLOTS))
                        rest(pool, pool_rests)
                        for k in range(K):
                            e = h * K + k
                            pool.indirect_dma_start(
                                out=rows[:, h % SLOTS, k, :], out_offset=None, in_=table_d,
                                in_offset=bass.IndirectOffsetOnAxis(ap=idx[:, par, e:e + 1], axis=0),
                            ).then_inc(gathered[h % SLOTS], 16)
                tiles(pool, step)

            @block.tensor
            def _(pe):
                def route(n, par):
                    pe.wait_ge(x2_in[par], 8 * (n - par) + 16)
                    if not (isinstance(n, int) and n < 1):
                        pe.wait_ge(xn_ready, n)
                    for c in range(CC):
                        mm = pe.transpose(ps_xT[:, c, :], x2_sb[:, par, c * P:(c + 1) * P], ident[:, :])
                    mm.then_inc(xT_mm, 1)
                    pe.wait_ge(xn_ready, n + 1)
                    if not (isinstance(n, int) and n < 1):
                        pe.wait_ge(scores_read, n)
                    for s in range(2):
                        for c in range(CC):
                            mm = pe.matmul(ps_score[s][:, :], xnT[:, c, :], keymap[:, c, s * 512:(s + 1) * 512],
                                           start=(c == 0), stop=(c == CC - 1))
                    mm.then_inc(score_mm, 1)

                def step(n, par):
                    for h in range(NH):
                        if h == 1 and not (isinstance(n, int) and n == TILES - 1):
                            route(n + 1, 1 - par)
                        pe.wait_ge(diag_ready, n * NH + (h + 1))
                        if h == 0 and not (isinstance(n, int) and n < 2):
                            pe.wait_ge(sum3_done, n - 1)
                        for k in range(K):
                            mm = pe.matmul(ps_out[par], diag[:, h % 2, k, :], rows[:, h % SLOTS, k, C:W2],
                                           start=(h == 0 and k == 0), stop=(h == NH - 1 and k == K - 1))
                        mm.then_inc(chunk_done, 1)
                route(0, 0)
                tiles(pe, step)

            @block.scalar
            def _(act):
                def route(n, par):
                    act.wait_ge(x2_in[par], 8 * (n - par) + 16)
                    if not (isinstance(n, int) and n < 2):
                        act.wait_ge(hid_ready, NH * (n - 1))
                    act.activation(ps_x2[par], x2_sb[:, par], ACT.Copy).then_inc(x2c_ready, 1)
                    act.wait_ge(xT_mm, n + 1)
                    if not (isinstance(n, int) and n < 1):
                        act.wait_ge(score_mm, n)
                    for c in range(CC):
                        last = act.activation(xnT[:, c, :], ps_xT[:, c, :], ACT.Identity, scale=bn_scale[:, c:c + 1],
                                              bias=bn_shift[:, c:c + 1])
                    last.then_inc(xn_ready, 1)

                def gates(n, par):
                    act.wait_ge(idx_ready, n + 1)
                    if not (isinstance(n, int) and n < 2):
                        act.wait_ge(coef_ready, NH * (n - 1))
                    act.activation(gate[:, par, :], sel[:, :, :].rearrange("p h k -> p (h k)"), ACT.Sigmoid)\
                        .then_inc(gate_ready, 1)

                def gelu(n, par, h):
                    act.wait_ge(hid_ready, n * NH + (h + 1))
                    act.activation(gel[:, par, h * K:(h + 1) * K], hid[:, par, h * K:(h + 1) * K], ACT.Gelu)\
                        .then_inc(gelu_ready, 1)

                def diags(n, par, h):
                    act.wait_ge(coef_ready, n * NH + (h + 1))
                    if not (isinstance(n, int) and n * NH + h < 2):
                        act.wait_ge(chunk_done, n * NH + (h - 1))
                    for k in range(K):
                        last = act.activation(diag[:, h % 2, k, :], ident[:, :], ACT.Copy,
                                              scale=coef[:, par, h * K + k:h * K + k + 1])
                    last.then_inc(diag_ready, 1)

                def std(n, par):
                    act.wait_ge(var3_ready, n + 1)
                    act.activation(sd3[:, :], mv3[:, 1:2], ACT.Sqrt, bias=eps_col[:, :]).then_inc(std3_ready, 1)
                act.wait_ge(norm_ready, 1)
                route(0, 0)
                gates(0, 0)

                def step(n, par):
                    more = not (isinstance(n, int) and n == TILES - 1)
                    for h in range(NH):
                        gelu(n, par, h)
                        diags(n, par, h)
                        if h == 1:
                            if not (isinstance(n, int) and n < 1):
                                std(n - 1, 1 - par)
                            if more:
                                route(n + 1, 1 - par)
                        if h == ROUTE_AT and more:
                            gates(n + 1, 1 - par)
                tiles(act, step)
                std(TILES - 1, 1)

            @block.vector
            def _(dve):
                def route(n, par):
                    dve.wait_ge(score_mm, n + 1)
                    if not (isinstance(n, int) and n < 1):
                        dve.wait_ge(gate_ready, n)
                    rest(dve, dve_rests)
                    def score(p, h):
                        return ps_score[p][:, h * NK:(h + 1) * NK]
                    for p in range(2):
                        for h in range(NH):
                            dve.max(out=top[:, p, h, :], in_=score(p, h))
                    dve.drain()
                    for p in range(2):
                        for h in range(NH):
                            last = dve.max_index(out=top_i[:, p, h, :], in_max=top[:, p, h, :], in_values=score(p, h))
                    last.then_inc(scores_read, 1)
                    dve.tensor_tensor(pair[:, :, :, :], top[:, 0, :, :, None].to_broadcast([P, NH, K, K]),
                                      top[:, 1, :, None, :].to_broadcast([P, NH, K, K]), ALU.add)
                    dve.drain()
                    for h in range(NH):
                        dve.max(out=sel[:, h, :], in_=pair[:, h, :, :].rearrange("p a b -> p (a b)"))
                    dve.drain()
                    for h in range(NH):
                        dve.max_index(out=sel_i[:, h, :], in_max=sel[:, h, :],
                                      in_values=pair[:, h, :, :].rearrange("p a b -> p (a b)"))
                    dve.drain()
                    flat_i = sel_i[:, :, :].rearrange("p h k -> p (h k)")
                    dve.tensor_scalar(half_i[:, 0, :], flat_i, 3, None, ALU.logical_shift_right)
                    dve.tensor_scalar(half_i[:, 1, :], flat_i, K - 1, None, ALU.bitwise_and)
                    dve.drain()
                    for p in range(2):
                        dve.tensor_tensor(hot[:, p], half_i[:, p, :, None].to_broadcast([P, HK, K]),
                                          iota8[:, None, :].to_broadcast([P, HK, K]), ALU.is_equal)
                    dve.drain()
                    for p in range(2):
                        h4 = hot[:, p].rearrange("p (h k) j -> p h k j", h=NH)
                        dve.tensor_tensor(h4, h4, top_i[:, p, :, None, :].to_broadcast([P, NH, K, K]), ALU.mult)
                    dve.drain()
                    for p in range(2):
                        dve.tensor_reduce(half_key[:, p, :], hot[:, p], AX.X, ALU.add)
                    dve.drain()
                    dve.scalar_tensor_tensor(out=idx[:, par, :], in0=half_key[:, 0, :], scalar=float(NK),
                                             in1=half_key[:, 1, :], op0=ALU.mult, op1=ALU.add).then_inc(idx_ready, 1)

                def hidden(n, par, h):
                    dve.wait_ge(gathered[h % SLOTS], n * (2 * 16 * K) + 16 * K * (h // SLOTS + 1))
                    for k in range(K):
                        last = dve.tensor_tensor_reduce(
                            out=rows[:, h % SLOTS, k, 0:C], in0=rows[:, h % SLOTS, k, 0:C], in1=ps_x2[par], scale=1.0, scalar=0.0,
                            op0=ALU.mult, op1=ALU.add, accum_out=hid[:, par, h * K + k:h * K + k + 1])
                    last.then_inc(hid_ready, 1)

                def coefs(n, par, h):
                    dve.wait_ge(gelu_ready, n * NH + (h + 1))
                    s = slice(h * K, (h + 1) * K)
                    dve.tensor_tensor(coef[:, par, s], gel[:, par, s], gate[:, par, s], ALU.mult)\
                        .then_inc(coef_ready, 1)

                def norm(n, par):
                    dve.wait_ge(chunk_done, NH * (n + 1))
                    dve.tensor_tensor(y3[:, :], ps_out[par], x2_sb[:, par], ALU.add).then_inc(sum3_done, 1)
                    dve.drain()
                    dve.bn_stats(out=st3[:, :], in_=y3[:, :])
                    dve.drain()
                    dve.bn_aggr(out=mv3[:, :], in_=st3[:, :]).then_inc(var3_ready, 1)

                def scale(n, par):
                    dve.wait_ge(std3_ready, n + 1)
                    dve.reciprocal(rs3[:, :], sd3[:, :])
                    dve.drain()
                    if not (isinstance(n, int) and n < 2):
                        dve.wait_ge(y_out[par], 8 * (n - par))
                    dve.tensor_scalar(yo[:, par, :], y3[:, :], mv3[:, 0:1], rs3[:, :], ALU.subtract, ALU.mult)\
                        .then_inc(y_ready, 1)
                route(0, 0)

                def step(n, par):
                    old = not (isinstance(n, int) and n < 1)
                    more = not (isinstance(n, int) and n == TILES - 1)
                    dve.wait_ge(x2c_ready, n + 1)
                    dve.wait_ge(gate_ready, n + 1)
                    for h in range(NH):
                        hidden(n, par, h)
                        coefs(n, par, h)
                        if h == 0 and old:
                            norm(n - 1, 1 - par)
                        if h == 2 and old:
                            scale(n - 1, 1 - par)
                        if h == ROUTE_AT and more:
                            route(n + 1, 1 - par)
                tiles(dve, step)
                norm(TILES - 1, 1)
                scale(TILES - 1, 1)


def kernel(x, ctx_1024, L0_attn_qkv_w, L0_attn_qkv_b, L0_attn_proj_w, L0_attn_proj_b, L0_ffn_bn_gamma,
           L0_ffn_bn_beta, L0_ffn_w_q, L0_ffn_keys_p, L0_ffn_down, L0_ffn_up):
    import numpy as np
    import concourse.bacc as bacc
    from concourse import mybir
    from concourse.bass_utils import run_bass_kernel_spmd as run

    B, T, C = x.shape
    a = lambda v: np.ascontiguousarray(np.asarray(v))
    x, ctx_1024 = a(x), a(ctx_1024)
    hs = L0_attn_qkv_w.shape[0] // 3
    flat = x.reshape(B * T, C)
    kp = a(L0_ffn_keys_p)
    ins = {
        "x": flat,
        "xT": a(flat.T),
        "ctx_rows": ctx_1024,
        "ctx_cols": a(ctx_1024.transpose(2, 0, 1)),
        "wqkvT": a(a(L0_attn_qkv_w).T),
        "bqkv": a(L0_attn_qkv_b).reshape(3 * hs, 1),
        "projT": a(a(L0_attn_proj_w).reshape(C, C // hs, hs).transpose(2, 0, 1)).reshape(hs, C * (C // hs)),
        "projb": a(L0_attn_proj_b).reshape(1, C),
        "gamma": a(a(L0_ffn_bn_gamma).reshape(C // 128, 128).T),
        "beta": a(a(L0_ffn_bn_beta).reshape(C // 128, 128).T),
        "wq": a(L0_ffn_w_q),
        "keysT": a(kp.transpose(3, 2, 0, 1)).reshape(kp.shape[3], 2 * kp.shape[0], kp.shape[1]),
        "table": np.concatenate([a(L0_ffn_down), a(L0_ffn_up)], axis=1),
    }
    nc = bacc.Bacc("TRN2", target_bir_lowering=False, num_devices=1)
    arrays, args = {}, []
    for name, v in ins.items():
        arrays[f"in_{name}"] = v
        args.append(nc.dram_tensor(f"in_{name}", v.shape, mybir.dt.from_np(v.dtype), kind="ExternalInput").ap())
    args.append(nc.dram_tensor("out_y", (B * T, C), mybir.dt.float32, kind="ExternalOutput").ap())
    decoder_layer(nc, *args)
    r = run(nc, [arrays], core_ids=[0])
    return r.results[0]["out_y"].reshape(B, T, C)
```

```python
from contextlib import ExitStack

import concourse.bass as bass
from concourse import mybir

F32 = mybir.dt.float32
I32 = mybir.dt.int32
U32 = mybir.dt.uint32
ALU = mybir.AluOpType
ACT = mybir.ActivationFunctionType
AX = mybir.AxisListType

P = 128
BIG = 1e30
TINY = 1e-30
EPS = 1e-5


def decoder_layer(nc, x, xT, ctx_rows_d, ctx_cols_d, wqkvT_d, bqkv_d, projT_d, projb_d, gamma_d, beta_d, wq_d,
                  keysT_d, table_d, out_d):
    NB, S2, C = ctx_rows_d.shape
    T = x.shape[0] // NB
    NT = T // P
    CC = C // P
    HS = wqkvT_d.shape[1] // 3
    NHEAD = C // HS
    TILES = x.shape[0] // P
    KD, NPH, NK = keysT_d.shape
    NH = NPH // 2
    K = 8
    NE, W2 = table_d.shape
    NG = 4
    RG = (S2 + NG - 1) // NG
    RP = NG * RG
    W = T + 1
    SLOTS = 4
    assert NB == P // NG and C == T == 2 * P and W2 == 2 * C and NK == 64 and KD == P and NH == 2 * SLOTS

    ctx = ExitStack()
    with ctx:
        def sb(name, shape, dt=F32):
            return ctx.enter_context(nc.sbuf_tensor(name, shape, dt))

        def sem(name):
            return ctx.enter_context(nc.semaphore(name))

        x1_d = nc.dram_tensor("x1_scratch", (x.shape[0], C), F32, kind="Internal").ap()
        x2_d = nc.dram_tensor("x2_scratch", (x.shape[0], C), F32, kind="Internal").ap()
        dist_d = nc.dram_tensor("dist_scratch", (NB, RP * T), F32, kind="Internal").ap()

        bank = [ctx.enter_context(nc.psum_tensor(f"bank{i}", [P, 512], F32)) for i in range(8)]

        ident = sb("ident", [P, P])
        iota_i = sb("iota_i", [P, T], I32)
        iota = sb("iota", [P, T])
        iota8 = sb("iota8", [P, K])
        causal = sb("causal", [P, NT, P])
        ones = sb("ones", [P, RP])
        fold = sb("fold", [P, NB])
        wqk = sb("wqk", [P, CC, 48])
        wv = sb("wv", [P, CC, HS])
        bias_qk = sb("bias_qk", [48, 1])
        bias_v = sb("bias_v", [P, HS])
        proj = sb("proj", [HS + 1, C])
        gamma = sb("gamma", [P, CC])
        beta = sb("beta", [P, CC])
        keymap = sb("keymap", [P, CC, NPH * NK])
        ctx_rows = sb("ctx_rows", [RP, NB, C])
        ctx_norm = sb("ctx_norm", [RP, NB])
        bn = sb("bn", [P, CC, NB, 6])
        bn_mv = sb("bn_mv", [P, CC, 2])
        bn_scale = sb("bn_scale", [P, CC])
        bn_shift = sb("bn_shift", [P, CC])
        bn_tmp = sb("bn_tmp", [P, CC])
        eps_col = sb("eps_col", [P, 1])

        w_in = sem("w_in")
        wq_in = sem("wq_in")
        ctx_in = [sem(f"ctx_in{i}") for i in range(NB // 8)]
        consts = sem("consts")
        setup_v = sem("setup_v")
        keymap_mm = sem("keymap_mm")
        keymap_done = sem("keymap_done")
        x_in = [sem(f"x_in{i}") for i in range(2)]
        p_in = sem("p_in")
        xT_in = [sem(f"xT_in{i}") for i in range(2)]
        qkv_mm = sem("qkv_mm")
        qk_ready = sem("qk_ready")
        v_ready = sem("v_ready")
        wei_mm = sem("wei_mm")
        weid_ready = sem("weid_ready")
        weio_ready = sem("weio_ready")
        head_mm = sem("head_mm")
        head_ready = sem("head_ready")
        attn_mm = sem("attn_mm")
        sum_done = sem("sum_done")
        var_ready = sem("var_ready")
        std_ready = sem("std_ready")
        x1_ready = sem("x1_ready")
        x1_out = [sem(f"x1_out{i}") for i in range(2)]
        x1T_mm = sem("x1T_mm")
        x1T_ready = sem("x1T_ready")
        ctxm2_ready = sem("ctxm2_ready")
        sq_ready = sem("sq_ready")
        dist_mm = sem("dist_mm")
        dist_ready = sem("dist_ready")
        root_ready = sem("root_ready")
        dist_out = [sem(f"dist_out{i}") for i in range(2)]
        cost_in = [sem(f"cost_in{g}") for g in range(NG)]
        table_init = sem("table_init")
        path_init = sem("path_init")
        path_done = sem("path_done")
        bounds_mm = sem("bounds_mm")
        bounds_ready = sem("bounds_ready")
        x1_in = [sem(f"x1_in{i}") for i in range(2)]
        mask_ready = sem("mask_ready")
        warp_mm = sem("warp_mm")
        sum2_done = sem("sum2_done")
        shift2_ready = sem("shift2_ready")
        var2_ready = sem("var2_ready")
        std2_ready = sem("std2_ready")
        x2_ready = sem("x2_ready")
        x2_out = [sem(f"x2_out{i}") for i in range(2)]
        x2T_mm = sem("x2T_mm")
        bn_done = sem("bn_done")
        bnvar_ready = sem("bnvar_ready")
        bnstd_ready = sem("bnstd_ready")
        norm_ready = sem("norm_ready")
        pool_rests, dve_rests, act_rests = sem("pool_rests"), sem("dve_rests"), sem("act_rests")
        x2_in = [sem(f"x2_in{i}") for i in range(2)]
        x2c_ready = sem("x2c_ready")
        xT_mm = sem("xT_mm")
        xn_ready = sem("xn_ready")
        score_mm = sem("score_mm")
        scores_read = sem("scores_read")
        idx_ready = sem("idx_ready")
        gate_ready = sem("gate_ready")
        gathered = [sem(f"gathered{i}") for i in range(SLOTS)]
        hid_ready = sem("hid_ready")
        gelu_ready = sem("gelu_ready")
        coef_ready = sem("coef_ready")
        diag_ready = sem("diag_ready")
        chunk_done = sem("chunk_done")
        sum3_done = sem("sum3_done")
        var3_ready = sem("var3_ready")
        std3_ready = sem("std3_ready")
        y_ready = sem("y_ready")
        y_out = [sem(f"y_out{i}") for i in range(2)]

        def rest(eng, spare):
            eng.sem_inc(spare, 1)

        def later(b, n):
            return not (isinstance(b, int) and b < n)

        def pipeline(eng, stages, peel, total=NB):
            def step(i, par):
                for stage, lag in stages:
                    if lag is None:
                        stage()
                        continue
                    b = i - lag
                    if not isinstance(b, int) or 0 <= b < total:
                        stage(b, (par + lag) % 2)
            for i in range(peel):
                step(i, i % 2)
            with eng.Fori(peel // 2, total // 2) as j:
                for par in range(2):
                    step(2 * j + par, par)
            for i in range(total, total + max(lag or 0 for _, lag in stages)):
                step(i, i % 2)

        def dmas(b, par):
            return 8 * (b - par) + 16

        with ExitStack() as st:
            def sa(name, shape, dt=F32):
                return st.enter_context(nc.sbuf_tensor(name, shape, dt))

            projT = sa("projT", [HS, C * NHEAD])
            ctx_cols = sa("ctx_cols", [P, CC, NB, S2])
            ctxm2 = sa("ctxm2", [P, 2, CC, RP])
            x_sb = sa("x_sb", [P, 2, NT, C])
            xT_sb = sa("xT_sb", [P, 2, CC, T])
            qT = sa("qT", [HS, 2, T])
            kT = sa("kT", [HS, 2, T])
            v_sb = sa("v_sb", [P, 2, NT, HS])
            weiT = sa("weiT", [P, 2, 3, P])
            headT = sa("headT", [HS + 1, 2, T])
            y1 = sa("y1", [P, 2, NT, C])
            st1 = sa("st1", [P, 2, NT, 6])
            mv1 = sa("mv1", [P, 2, NT, 2])
            sd1 = sa("sd1", [P, 2, NT])
            rs1 = sa("rs1", [P, 2, NT])
            x1_sb = sa("x1_sb", [P, 2, NT, C])
            x1T = sa("x1T", [P, 2, CC, T])
            x1sq = sa("x1sq", [P, CC, T])
            x1sum = sa("x1sum", [P, 2, T])
            dist_sb = sa("dist_sb", [RP, 2, T])
            sq_scr = sa("sq_scr", [RP, 8, C])

            ps_qk, ps_v = bank[0][0:48, 0:T], bank[6][:, 0:NT * HS].rearrange("p (t d) -> p t d", t=NT)
            ps_wei = bank[1][:, 0:3 * P].rearrange("p (k t) -> p k t", k=3)
            ps_head = bank[2][0:HS, 0:T]
            ps_attn = bank[3][:, :].rearrange("p (t c) -> p t c", t=NT)
            ps_x1T = bank[4][:, :].rearrange("p (c t) -> p c t", c=CC)
            ps_dist = bank[5][0:RP, 0:T]

            block = st.enter_context(nc.Block())
            xb = x.rearrange("(b t p) c -> b p t c", b=NB, t=NT)
            x1b = x1_d.rearrange("(b t p) c -> b p t c", b=NB, t=NT)
            xTb = xT.rearrange("(k p) (b t) -> b p k t", k=CC, b=NB)

            @block.sync
            def _(sp):
                def one(ap, b):
                    return ap[bass.ds(b, 1)].rearrange("a p t c -> (a p) t c")

                def load_xT(b, par):
                    if isinstance(b, int) and b == 1:
                        for dst, src in ((projT[:, :], projT_d), (proj[HS:HS + 1, :], projb_d),
                                         (gamma[:, :], gamma_d), (beta[:, :], beta_d)):
                            sp.dma_start(dst, src).then_inc(p_in, 16)
                    if isinstance(b, int) and 2 <= b < 2 + NB // 8:
                        if b == 2:
                            sp.wait_ge(consts, 6)
                        some = slice(8 * (b - 2), 8 * (b - 1))
                        sp.dma_start(ctx_rows[0:S2, some, :], ctx_rows_d[some].rearrange("b s c -> s b c"))\
                            .then_inc(ctx_in[b - 2], 16)
                        sp.dma_start(ctx_cols[:, :, some, :],
                                     ctx_cols_d[:, some].rearrange("(k p) b s -> p k b s", k=CC))\
                            .then_inc(ctx_in[b - 2], 16)
                    if later(b, 2):
                        sp.wait_ge(qkv_mm, b - 1)
                    sp.dma_start(xT_sb[:, par], one(xTb, b)).then_inc(xT_in[par], 16)

                def load_x(b, par):
                    if later(b, 2):
                        sp.wait_ge(sum_done, b - 1)
                    sp.dma_start(x_sb[:, par], one(xb, b)).then_inc(x_in[par], 16)

                def store_x1(b, par):
                    sp.wait_ge(x1_ready, b + 1)
                    sp.dma_start(one(x1b, b), x1_sb[:, par]).then_inc(x1_out[par], 16)

                def store_dist(b, par):
                    sp.wait_ge(root_ready, b + 1)
                    sp.dma_start(dist_d[bass.ds(b, 1)].rearrange("a (i j) -> (a i) j", i=RP),
                                 dist_sb[:, par]).then_inc(dist_out[par], 16)

                for dst, src in ((wqk[:, :, 0:HS], wqkvT_d[:, 0:HS].rearrange("(k p) d -> p k d", k=CC)),
                                 (wqk[:, :, 32:32 + HS], wqkvT_d[:, HS:2 * HS].rearrange("(k p) d -> p k d", k=CC)),
                                 (wv[:, :, :], wqkvT_d[:, 2 * HS:].rearrange("(k p) d -> p k d", k=CC)),
                                 (bias_qk[0:HS, :], bqkv_d[0:HS]), (bias_qk[32:32 + HS, :], bqkv_d[HS:2 * HS]),
                                 (bias_v[:, :], bqkv_d[2 * HS:].rearrange("d a -> a d").to_broadcast([P, HS]))):
                    sp.dma_start(dst, src).then_inc(w_in, 16)
                pipeline(sp, [(load_xT, 0), (load_x, 5), (store_x1, 7), (store_dist, 10)], 12)
                for par in range(2):
                    sp.wait_ge(x1_out[par], 16 * NB // 2)
                    sp.wait_ge(dist_out[par], 16 * NB // 2)

            @block.gpsimd
            def _(pool):
                pool.memset(wqk[:, :, HS:32], 0.0)
                pool.memset(ones[:, :], 1.0)
                pool.memset(headT[:, :, :], 1.0)
                pool.memset(ctxm2[:, :, :, :], 0.0)
                pool.memset(eps_col[:, :], EPS)
                pool.memset(ident[:, :], 0.0)
                pool.memset(causal[:, :, :], 1.0)
                pool.iota(iota_i[:, :], [[1, T]], base=0, channel_multiplier=0)
                pool.drain()
                pool.affine_select(out=ident[:, :], in_=ident[:, :], compare_op=ALU.not_equal, fill=1.0, base=0,
                                   pattern=[[-1, P]], channel_multiplier=1)
                pool.affine_select(out=causal[:, :, :], in_=causal[:, :, :], compare_op=ALU.is_ge, fill=0.0,
                                   base=0, pattern=[[0, NT], [1, P]], channel_multiplier=-1)
                pool.drain()
                pool.memset(ctx_rows[64:RP, :, :], 0.0)
                pool.drain()
                pool.nop().then_inc(consts, 6)

                def squares(b, par):
                    pool.wait_ge(x1T_ready, b + 1)
                    pool.tensor_tensor(x1sq[:, :, :], x1T[:, par], x1T[:, par], ALU.mult)
                    pool.drain()
                    if later(b, 2):
                        pool.wait_ge(dist_mm, b - 1)
                    pool.tensor_tensor(x1sum[:, par, :], x1sq[:, 0, :], x1sq[:, 1, :], ALU.add).then_inc(sq_ready, 1)
                    pool.drain()
                pipeline(pool, [(squares, 0)], 2)

            @block.tensor
            def _(pe):
                def qkv(b, par):
                    pe.wait_ge(xT_in[par], dmas(b, par))
                    if later(b, 1):
                        pe.wait_ge(qk_ready, b)
                        pe.wait_ge(v_ready, b)
                    for c in range(CC):
                        pe.matmul(ps_qk, wqk[:, c, :], xT_sb[:, par, c, :], start=(c == 0), stop=(c == CC - 1))
                    for t in range(NT):
                        for c in range(CC):
                            mm = pe.matmul(ps_v[:, t, :], xT_sb[:, par, c, t * P:(t + 1) * P], wv[:, c, :],
                                           start=(c == 0), stop=(c == CC - 1))
                    mm.then_inc(qkv_mm, 1)

                def wei(b, par):
                    pe.wait_ge(qk_ready, b + 1)
                    if later(b, 1):
                        pe.wait_ge(weio_ready, b)
                    pe.matmul(ps_wei[:, 0, :], kT[:, par, P:T], qT[:, par, P:T], start=True, stop=True)
                    pe.matmul(ps_wei[:, 1:3, :].rearrange("p k t -> p (k t)"), kT[:, par, 0:P], qT[:, par, :],
                              start=True, stop=True).then_inc(wei_mm, 1)

                def head(b, par):
                    pe.wait_ge(v_ready, b + 1)
                    pe.wait_ge(weid_ready, b + 1)
                    pe.wait_ge(weio_ready, b + 1)
                    if later(b, 1):
                        pe.wait_ge(head_ready, b)
                    pe.matmul(ps_head, v_sb[:, par, 0, :], weiT[:, par, 1:3, :].rearrange("p k t -> p (k t)"),
                              start=True, stop=False)
                    pe.matmul(ps_head[:, P:T], v_sb[:, par, 1, :], weiT[:, par, 0, :], start=False, stop=True)\
                        .then_inc(head_mm, 1)

                def attn(b, par):
                    pe.wait_ge(head_ready, b + 1)
                    if not later(b, 1):
                        pe.wait_ge(setup_v, 1)
                    if later(b, 1):
                        pe.wait_ge(sum_done, b)
                    for t in range(NT):
                        mm = pe.matmul(ps_attn[:, t, :], headT[:, par, t * P:(t + 1) * P], proj[:, :],
                                       start=True, stop=True)
                    mm.then_inc(attn_mm, 1)

                def turn_x1(b, par):
                    pe.wait_ge(x1_ready, b + 1)
                    if later(b, 1):
                        pe.wait_ge(x1T_ready, b)
                    for c in range(CC):
                        for t in range(NT):
                            mm = pe.transpose(ps_x1T[:, c, t * P:(t + 1) * P], x1_sb[:, par, t, c * P:(c + 1) * P],
                                              ident[:, :])
                    mm.then_inc(x1T_mm, 1)

                def dist(b, par):
                    pe.wait_ge(ctxm2_ready, b + 1)
                    pe.wait_ge(x1T_ready, b + 1)
                    if later(b, 1):
                        pe.wait_ge(dist_ready, b)
                    for c in range(CC):
                        pe.matmul(ps_dist, ctxm2[:, par, c, :], x1T[:, par, c, :], start=(c == 0), stop=False)
                    pe.wait_ge(sq_ready, b + 1)
                    pe.matmul(ps_dist, ones[:, :], x1sum[:, par, :], start=False, stop=True).then_inc(dist_mm, 1)

                pe.wait_ge(consts, 6)
                pe.wait_ge(w_in, 16 * 6)
                pipeline(pe, [(qkv, 0), (wei, 1), (head, 2), (attn, 3), (turn_x1, 6), (dist, 7)], 10)

            @block.scalar
            def _(act):
                def qk(b, par):
                    act.wait_ge(qkv_mm, b + 1)
                    if later(b, 2):
                        act.wait_ge(wei_mm, b - 1)
                    act.activation(qT[:, par, :], ps_qk[0:HS, :], ACT.Identity, bias=bias_qk[0:HS, :])
                    act.activation(kT[:, par, :], ps_qk[32:32 + HS, :], ACT.Identity, bias=bias_qk[32:32 + HS, :])\
                        .then_inc(qk_ready, 1)

                def wei_off(b, par):
                    act.wait_ge(weid_ready, b + 1)
                    act.wait_ge(wei_mm, b + 1)
                    if later(b, 2):
                        act.wait_ge(head_mm, b - 1)
                    act.activation(weiT[:, par, 2, :], ps_wei[:, 2, :], ACT.Copy).then_inc(weio_ready, 1)

                def x1_cols(b, par):
                    act.wait_ge(x1T_mm, b + 1)
                    if later(b, 2):
                        act.wait_ge(dist_mm, b - 1)
                        act.wait_ge(sq_ready, b - 1)
                    act.activation(x1T[:, par], ps_x1T[:, :, :], ACT.Copy).then_inc(x1T_ready, 1)

                def ctx_scale(b, par):
                    if not later(b, 1):
                        for part in ctx_in:
                            act.wait_ge(part, 32)
                    if later(b, 2):
                        act.wait_ge(dist_mm, b - 1)
                    rest(act, act_rests)
                    act.activation(ctxm2[:, par, :, 0:S2],
                                   ctx_cols[:, :, bass.ds(b, 1), :].rearrange("p k a s -> p k (a s)"),
                                   ACT.Copy, scale=-2.0).then_inc(ctxm2_ready, 1)

                def head(b, par):
                    act.wait_ge(head_mm, b + 1)
                    if later(b, 2):
                        act.wait_ge(attn_mm, b - 1)
                    act.activation(headT[0:HS, par, :], ps_head, ACT.Copy).then_inc(head_ready, 1)

                def std(b, par):
                    act.wait_ge(var_ready, b + 1)
                    act.activation(sd1[:, par, :], mv1[:, par, :, 1], ACT.Sqrt, bias=eps_col[:, :])\
                        .then_inc(std_ready, 1)

                def root(b, par):
                    act.wait_ge(dist_ready, b + 1)
                    act.activation(dist_sb[:, par, :], dist_sb[:, par, :], ACT.Sqrt).then_inc(root_ready, 1)

                act.wait_ge(consts, 6)
                act.wait_ge(w_in, 96)
                pipeline(act, [(root, 9), (qk, 0), (head, 2), (std, 4), (wei_off, 1), (ctx_scale, 6), (x1_cols, 6)], 12)

            @block.vector
            def _(dve):
                def v(b, par):
                    dve.wait_ge(qkv_mm, b + 1)
                    if later(b, 2):
                        dve.wait_ge(head_mm, b - 1)
                    dve.tensor_tensor(v_sb[:, par], ps_v, bias_v[:, None, :].to_broadcast([P, NT, HS]), ALU.add)\
                        .then_inc(v_ready, 1)

                def wei_diag(b, par):
                    dve.wait_ge(wei_mm, b + 1)
                    if later(b, 2):
                        dve.wait_ge(head_mm, b - 1)
                    dve.tensor_tensor(weiT[:, par, 0:2, :], ps_wei[:, 0:2, :], causal[:, :, :], ALU.mult)\
                        .then_inc(weid_ready, 1)

                def dist(b, par):
                    dve.wait_ge(dist_mm, b + 1)
                    if later(b, 2):
                        dve.wait_ge(dist_out[par], dmas(b, par) - 16)
                    dve.tensor_scalar(dist_sb[:, par, :], ps_dist, ctx_norm[:, bass.ds(b, 1)], TINY, ALU.add, ALU.max)\
                        .then_inc(dist_ready, 1)

                def residual(b, par):
                    dve.wait_ge(attn_mm, b + 1)
                    dve.wait_ge(x_in[par], dmas(b, par))
                    dve.tensor_tensor(y1[:, par], ps_attn, x_sb[:, par], ALU.add).then_inc(sum_done, 1)

                def recip(b, par):
                    dve.wait_ge(std_ready, b + 1)
                    dve.reciprocal(rs1[:, par, :], sd1[:, par, :])

                def settle():
                    dve.drain()

                def stats(b, par):
                    for t in range(NT):
                        dve.bn_stats(out=st1[:, par, t, :], in_=y1[:, par, t, :])

                def aggr(b, par):
                    for t in range(NT):
                        last = dve.bn_aggr(out=mv1[:, par, t, :], in_=st1[:, par, t, :])
                    last.then_inc(var_ready, 1)

                def scale(b, par):
                    if later(b, 2):
                        dve.wait_ge(x1_out[par], dmas(b, par) - 16)
                        dve.wait_ge(x1T_mm, b - 1)
                    for t in range(NT):
                        last = dve.tensor_scalar(x1_sb[:, par, t, :], y1[:, par, t, :], mv1[:, par, t, 0:1],
                                                 rs1[:, par, t:t + 1], ALU.subtract, ALU.mult)
                    last.then_inc(x1_ready, 1)

                def norms(b, par):
                    if isinstance(b, int) and b < NB // 8:
                        dve.wait_ge(ctx_in[b], 32)
                        for k in range(8 * b, 8 * b + 8):
                            dve.tensor_tensor_reduce(out=sq_scr[:, k % 8, :], in0=ctx_rows[:, k, :],
                                                     in1=ctx_rows[:, k, :], scale=1.0, scalar=0.0, op0=ALU.mult,
                                                     op1=ALU.add, accum_out=ctx_norm[:, k:k + 1])

                def setup(b, par):
                    if not later(b, 1):
                        dve.wait_ge(p_in, 64)
                        dve.tensor_reduce(proj[0:HS, :], projT[:, :].rearrange("d (c h) -> d c h", h=NHEAD), AX.X,
                                          ALU.add).then_inc(setup_v, 1)
                        dve.tensor_copy(iota[:, :], iota_i[:, :])
                        dve.tensor_copy(iota8[:, :], iota_i[:, 0:K])
                        dve.tensor_reduce(fold[:, :], ident[:, :].rearrange("p (g b) -> p b g", g=NG), AX.X, ALU.add)

                dve.wait_ge(consts, 6)
                dve.wait_ge(w_in, 96)
                pipeline(dve, [(residual, 4), (recip, 5), (v, 0), (wei_diag, 1), (setup, 1), (settle, None), (norms, 4),
                               (stats, 4), (dist, 8), (scale, 5), (settle, None), (aggr, 4)], 10)

        with ExitStack() as st:
            def sw(name, shape, dt=F32):
                return st.enter_context(nc.sbuf_tensor(name, shape, dt))

            cost = sw("cost", [P, RG * T])
            acc = sw("acc", [P, (RG + 1) * W])
            best = sw("best", [P, RG * T])
            is_left = sw("is_left", [P, RG * T])
            entry = sw("entry", [P, RG * T])
            picked = sw("picked", [P, 2, T])
            path = sw("path", [P, RG + 1])
            lo_hi = sw("lo_hi", [P, 2, RP])
            bounds = sw("bounds", [RP, 2, NB])
            wq_rows = sw("wq_rows", [P, NPH, C])
            keysT = sw("keysT", [P, NPH, NK])
            above = sw("above", [S2, 2, T])
            mask = sw("mask", [S2, 2, T])
            x1_sb = sw("x1_again", [P, 2, NT, C])
            y2 = sw("y2", [P, 2, NT, C])
            st2 = sw("st2", [P, 2, NT, 6])
            mv2 = sw("mv2", [P, 2, NT, 2])
            sd2 = sw("sd2", [P, 2, NT])
            rs2 = sw("rs2", [P, 2, NT])
            nb2 = sw("nb2", [P, 2, NT])
            x2_sb = sw("x2_sb", [P, 2, NT, C])
            ps_bounds = bank[0][0:RP, 0:2 * NB].rearrange("p (a b) -> p a b", a=2)
            ps_warp = [bank[1 + i][:, :].rearrange("p (t c) -> p t c", t=NT) for i in range(2)]
            ps_x2T = [bank[3 + i][:, :].rearrange("p (c t) -> p c t", c=CC) for i in range(2)]
            ps_key = [bank[4 + i] for i in range(4)]
            x1b = x1_d.rearrange("(b t p) c -> b p t c", b=NB, t=NT)
            x2b = x2_d.rearrange("(b t p) c -> b p t c", b=NB, t=NT)
            acc3 = acc[:, :].rearrange("p (r w) -> p r w", w=W)

            block = st.enter_context(nc.Block())

            @block.sync
            def _(sp):
                for g in range(NG):
                    sp.dma_start(cost[NB * g:NB * (g + 1), :], dist_d[:, RG * T * g:RG * T * (g + 1)])\
                        .then_inc(cost_in[g], 16)
                sp.dma_start(keysT[:, :, :], keysT_d).then_inc(wq_in, 16)
                sp.dma_start(wq_rows[:, :, :], wq_d.rearrange("(g d) c -> d g c", g=NPH)).then_inc(wq_in, 16)

                def one(ap, b):
                    return ap[bass.ds(b, 1)].rearrange("a p t c -> (a p) t c")

                def load(b, par):
                    if later(b, 2):
                        sp.wait_ge(sum2_done, b - 1)
                    sp.dma_start(x1_sb[:, par], one(x1b, b)).then_inc(x1_in[par], 16)

                def store(b, par):
                    sp.wait_ge(x2_ready, b + 1)
                    sp.dma_start(one(x2b, b), x2_sb[:, par]).then_inc(x2_out[par], 16)

                pipeline(sp, [(load, 0), (store, 3)], 6)
                for par in range(2):
                    sp.wait_ge(x2_out[par], 16 * NB // 2)

            @block.gpsimd
            def _(pool):
                pool.memset(acc[:, :], BIG)
                pool.drain()
                pool.memset(acc[0:NB, 0:1], 0.0)
                pool.memset(best[:, :], BIG)
                pool.memset(lo_hi[:, :, :], 0.0)
                pool.memset(path[:, :], 0.0)
                pool.drain()
                pool.nop().then_inc(table_init, 1)

            @block.scalar
            def _(act):
                act.wait_ge(keymap_mm, 1)
                for i in range(4):
                    kc = act.activation(keymap[:, i // 2, (i % 2) * 512:(i % 2 + 1) * 512], ps_key[i][:, :], ACT.Copy)
                kc.then_inc(keymap_done, 1)
                act.wait_ge(bounds_mm, 1)
                act.activation(bounds[:, :, :], ps_bounds, ACT.Copy).then_inc(bounds_ready, 1)

                def std(b, par):
                    act.wait_ge(var2_ready, b + 1)
                    act.activation(sd2[:, par, :], mv2[:, par, :, 1], ACT.Sqrt, bias=eps_col[:, :])\
                        .then_inc(std2_ready, 1)

                def norm(b, par):
                    act.wait_ge(shift2_ready, b + 1)
                    if later(b, 2):
                        act.wait_ge(x2_out[par], dmas(b, par) - 16)
                        act.wait_ge(x2T_mm, b - 1)
                    for t in range(NT):
                        last = act.activation(x2_sb[:, par, t, :], y2[:, par, t, :], ACT.Identity,
                                              scale=rs2[:, par, t:t + 1], bias=nb2[:, par, t:t + 1])
                    last.then_inc(x2_ready, 1)
                pipeline(act, [(norm, 3), (std, 2)], 6)
                act.wait_ge(bnvar_ready, 1)
                act.activation(bn_tmp[:, :], bn_mv[:, :, 1], ACT.Sqrt, bias=eps_col[:, :]).then_inc(bnstd_ready, 1)

            @block.tensor
            def _(pe):
                pe.wait_ge(wq_in, 32)
                for c in range(CC):
                    for g in range(NPH):
                        mm = pe.matmul(ps_key[2 * c + g // NH][:, (g % NH) * NK:(g % NH + 1) * NK],
                                       wq_rows[:, g, c * P:(c + 1) * P], keysT[:, g, :], start=True, stop=True)
                mm.then_inc(keymap_mm, 1)
                pe.wait_ge(path_done, 1)
                for a in range(2):
                    mm = pe.matmul(ps_bounds[:, a, :], lo_hi[:, a, :], fold[:, :], start=True, stop=True)
                mm.then_inc(bounds_mm, 1)

                def warp(b, par):
                    pe.wait_ge(mask_ready, b + 1)
                    if later(b, 2):
                        pe.wait_ge(sum2_done, b - 1)
                    for t in range(NT):
                        mm = pe.matmul(ps_warp[par][:, t, :], mask[:, par, t * P:(t + 1) * P],
                                       ctx_rows[0:S2, bass.ds(b, 1), :].rearrange("s a c -> s (a c)"),
                                       start=True, stop=True)
                    mm.then_inc(warp_mm, 1)

                def turn(b, par):
                    pe.wait_ge(x2_ready, b + 1)
                    if later(b, 2):
                        pe.wait_ge(bn_done, b - 1)
                    for c in range(CC):
                        for t in range(NT):
                            mm = pe.transpose(ps_x2T[par][:, c, t * P:(t + 1) * P],
                                              x2_sb[:, par, t, c * P:(c + 1) * P], ident[:, :])
                    mm.then_inc(x2T_mm, 1)
                pe.wait_ge(keymap_done, 1)
                pipeline(pe, [(turn, 4), (warp, 1)], 6)

            @block.vector
            def _(dve):
                dve.wait_ge(table_init, 1)
                for g in range(NG):
                    q = slice(NB * g, NB * (g + 1))
                    rows = min(RG, S2 - RG * g)
                    dve.wait_ge(cost_in[g], 16)
                    if g:
                        dve.tensor_copy(acc[q, 0:W], acc[NB * (g - 1):NB * g, RG * W:(RG + 1) * W])
                        dve.drain()

                    def row(r):
                        dve.tensor_tensor(best[q, bass.ds(r * T, T)], acc[q, bass.ds(r * W + 1, T)],
                                          acc[q, bass.ds(r * W, T)], ALU.min)
                        dve.drain()
                        dve.tensor_tensor_scan(acc[q, bass.ds(r * W + W + 1, T)], best[q, bass.ds(r * T, T)],
                                               cost[q, bass.ds(r * T, T)], BIG, ALU.min, ALU.add)
                        dve.drain()
                    U = 10
                    if rows // U > 1:
                        with dve.Fori(0, rows // U) as i:
                            for u in range(U):
                                row(i * U + u)
                    for r in range(rows // U * U if rows // U > 1 else 0, rows):
                        row(r)

                best3 = best[:, :].rearrange("p (r t) -> p r t", t=T)
                left3 = is_left[:, :].rearrange("p (r t) -> p r t", t=T)
                entry3 = entry[:, :].rearrange("p (r t) -> p r t", t=T)
                dve.tensor_tensor(left3, acc3[:, 1:, 0:T], best3, ALU.is_lt)
                dve.tensor_tensor(entry3, acc3[:, 0:RG, 0:T], acc3[:, 0:RG, 1:W], ALU.is_le)
                dve.drain()
                dve.scalar_tensor_tensor(out=best3, in0=entry3, scalar=-0.75,
                                         in1=iota[:, None, :].to_broadcast([P, RG, T]), op0=ALU.mult, op1=ALU.add)
                dve.drain()
                dve.scalar_tensor_tensor(out=best[:, :], in0=is_left[:, :], scalar=-1.0, in1=best[:, :],
                                         op0=ALU.add, op1=ALU.mult)
                dve.drain()
                dve.tensor_tensor_scan(entry[:, :], is_left[:, :], best[:, :], 0.0, ALU.mult, ALU.subtract)

                dve.drain()
                dve.tensor_copy(best3[:, :, 0:1], entry3[:, :, 0:1])
                dve.tensor_tensor(best3[:, :, 1:T], entry3[:, :, 1:T], entry3[:, :, 0:T - 1], ALU.subtract)

                def climb(q, r, par):
                    dve.scalar_tensor_tensor(out=picked[q, par, :], in0=iota[q, :], scalar=path[q, bass.ds(r + 1, 1)],
                                             in1=best[q, bass.ds(r * T, T)], op0=ALU.is_le, op1=ALU.mult,
                                             accum_out=path[q, bass.ds(r, 1)])
                    dve.drain()
                for g in range(NG - 1, -1, -1):
                    q, rows = slice(NB * g, NB * (g + 1)), min(RG, S2 - RG * g)
                    if g == NG - 1:
                        dve.memset(path[q, rows:rows + 1], float(T - 1))
                    else:
                        dve.tensor_copy(path[q, RG:RG + 1], path[NB * (g + 1):NB * (g + 2), 0:1])
                    dve.drain()
                    U = 10
                    if rows // U > 1:
                        with dve.Fori(0, rows // U) as j:
                            for u in range(U):
                                climb(q, j * -U + (rows - 1 - u), u % 2)
                    for r in range(rows - 1 - (rows // U * U if rows // U > 1 else 0), -1, -1):
                        climb(q, r, r % 2)
                for g in range(NG):
                    q, rows = slice(NB * g, NB * (g + 1)), min(RG, S2 - RG * g)
                    for a in range(2):
                        dve.tensor_copy(lo_hi[q, a, RG * g:RG * g + rows], path[q, a:a + rows])
                dve.drain()
                dve.nop().then_inc(path_done, 1)
                dve.wait_ge(bounds_ready, 1)

                def masks_above(b, par):
                    dve.tensor_scalar(above[:, par, :], iota[0:S2, :], bounds[0:S2, 0, bass.ds(b, 1)], None, ALU.is_ge)

                def masks(b, par):
                    if later(b, 2):
                        dve.wait_ge(warp_mm, b - 1)
                    dve.scalar_tensor_tensor(out=mask[:, par, :], in0=iota[0:S2, :],
                                             scalar=bounds[0:S2, 1, bass.ds(b, 1)], in1=above[:, par, :],
                                             op0=ALU.is_le, op1=ALU.mult).then_inc(mask_ready, 1)

                def add(b, par):
                    dve.wait_ge(warp_mm, b + 1)
                    dve.wait_ge(x1_in[par], dmas(b, par))
                    if later(b, 2):
                        dve.wait_ge(x2_ready, b - 1)
                    dve.tensor_tensor(y2[:, par], ps_warp[par], x1_sb[:, par], ALU.add).then_inc(sum2_done, 1)

                def stats(b, par):
                    for t in range(NT):
                        dve.bn_stats(out=st2[:, par, t, :], in_=y2[:, par, t, :])

                def aggr(b, par):
                    for t in range(NT):
                        last = dve.bn_aggr(out=mv2[:, par, t, :], in_=st2[:, par, t, :])
                    last.then_inc(var2_ready, 1)

                def recip(b, par):
                    dve.wait_ge(std2_ready, b + 1)
                    dve.reciprocal(rs2[:, par, :], sd2[:, par, :])

                def shift(b, par):
                    dve.scalar_tensor_tensor(out=nb2[:, par, :], in0=mv2[:, par, :, 0], scalar=-1.0,
                                             in1=rs2[:, par, :], op0=ALU.mult, op1=ALU.mult)\
                        .then_inc(shift2_ready, 1)

                def chan_stats(b, par):
                    dve.wait_ge(x2T_mm, b + 1)
                    for c in range(CC):
                        last = dve.bn_stats(out=bn[:, c, bass.ds(b, 1), :].rearrange("p a s -> p (a s)"),
                                            in_=ps_x2T[par][:, c, :])
                    last.then_inc(bn_done, 1)

                def settle():
                    dve.drain()
                pipeline(dve, [(masks_above, 0), (add, 2), (recip, 3), (settle, None), (masks, 0), (shift, 3), (chan_stats, 5),
                               (stats, 2), (settle, None), (aggr, 2)], 8)
                dve.drain()
                for c in range(CC):
                    last = dve.bn_aggr(out=bn_mv[:, c, :], in_=bn[:, c, :, :].rearrange("p b s -> p (b s)"))
                last.then_inc(bnvar_ready, 1)
                dve.wait_ge(bnstd_ready, 1)
                dve.reciprocal(bn_scale[:, :], bn_tmp[:, :])
                dve.drain()
                dve.tensor_tensor(bn_scale[:, :], bn_scale[:, :], gamma[:, :], ALU.mult)
                dve.drain()
                dve.tensor_tensor(bn_tmp[:, :], bn_mv[:, :, 0], bn_scale[:, :], ALU.mult)
                dve.drain()
                dve.tensor_tensor(bn_shift[:, :], beta[:, :], bn_tmp[:, :], ALU.subtract).then_inc(norm_ready, 1)

        with ExitStack() as st:
            def se(name, shape, dt=F32):
                return st.enter_context(nc.sbuf_tensor(name, shape, dt))

            HK = NH * K
            x2_sb = se("x2_tile", [P, 2, C])
            xnT = se("xnT", [P, CC, P])
            top = se("top", [P, 2, NH, K])
            top_i = se("top_i", [P, 2, NH, K], U32)
            pair = se("pair", [P, NH, K, K])
            sel = se("sel", [P, NH, K])
            sel_i = se("sel_i", [P, NH, K], U32)
            half_i = se("half_i", [P, 2, HK], U32)
            hot = se("hot", [P, 2, HK, K])
            half_key = se("half_key", [P, 2, HK])
            idx = se("idx", [P, 2, HK], U32)
            gate = se("gate", [P, 2, HK])
            rows = se("rows", [P, SLOTS, K, W2])
            hid = se("hid", [P, 2, HK])
            gel = se("gel", [P, 2, HK])
            coef = se("coef", [P, 2, HK])
            diag = se("diag", [P, 2, K, P])
            y3 = se("y3", [P, C])
            st3 = se("st3", [P, 6])
            mv3 = se("mv3", [P, 2])
            sd3 = se("sd3", [P, 1])
            rs3 = se("rs3", [P, 1])
            yo = se("yo", [P, 2, C])
            ps_score = bank[0], bank[1]
            ps_xT = bank[2][:, 0:C].rearrange("p (c t) -> p c t", c=CC)
            ps_x2 = [bank[3][:, 0:C], bank[4][:, 0:C]]
            ps_out = [bank[5][:, 0:C], bank[6][:, 0:C]]
            x2t = x2_d.rearrange("(n p) c -> n p c", p=P)
            outt = out_d.rearrange("(n p) c -> n p c", p=P)
            ROUTE_AT = 3

            def tiles(eng, step):
                for n in range(2):
                    step(n, n)
                with eng.Fori(1, TILES // 2 - 1) as j:
                    for par in range(2):
                        step(2 * j + par, par)
                for n in range(TILES - 2, TILES):
                    step(n, n % 2)

            block = st.enter_context(nc.Block())

            @block.sync
            def _(sp):
                def load(n, par):
                    if not (isinstance(n, int) and n < 2):
                        sp.wait_ge(sum3_done, n - 1)
                        sp.wait_ge(xT_mm, n - 1)
                        sp.wait_ge(x2c_ready, n - 1)
                    sp.dma_start(x2_sb[:, par], x2t[bass.ds(n, 1)].rearrange("a p c -> (a p) c"))\
                        .then_inc(x2_in[par], 16)

                def store(n, par):
                    sp.wait_ge(y_ready, n + 1)
                    sp.dma_start(outt[bass.ds(n, 1)].rearrange("a p c -> (a p) c"), yo[:, par])\
                        .then_inc(y_out[par], 16)
                load(0, 0)

                def step(n, par):
                    if not (isinstance(n, int) and n < 1):
                        pass
                    if not (isinstance(n, int) and n == TILES - 1):
                        load(n + 1, 1 - par)
                    if not (isinstance(n, int) and n < 1):
                        store(n - 1, 1 - par)
                tiles(sp, step)
                store(TILES - 1, 1)
                for par in range(2):
                    sp.wait_ge(y_out[par], 16 * TILES // 2)

            @block.gpsimd
            def _(pool):
                def step(n, par):
                    pool.wait_ge(idx_ready, n + 1)
                    for h in range(NH):
                        if not (isinstance(n, int) and n * NH + h < SLOTS):
                            pool.wait_ge(chunk_done, n * NH + (h + 1 - SLOTS))
                        rest(pool, pool_rests)
                        for k in range(K):
                            e = h * K + k
                            pool.indirect_dma_start(
                                out=rows[:, h % SLOTS, k, :], out_offset=None, in_=table_d,
                                in_offset=bass.IndirectOffsetOnAxis(ap=idx[:, par, e:e + 1], axis=0),
                            ).then_inc(gathered[h % SLOTS], 16)
                tiles(pool, step)

            @block.tensor
            def _(pe):
                def route(n, par):
                    pe.wait_ge(x2_in[par], 8 * (n - par) + 16)
                    if not (isinstance(n, int) and n < 1):
                        pe.wait_ge(xn_ready, n)
                    for c in range(CC):
                        mm = pe.transpose(ps_xT[:, c, :], x2_sb[:, par, c * P:(c + 1) * P], ident[:, :])
                    mm.then_inc(xT_mm, 1)
                    pe.wait_ge(xn_ready, n + 1)
                    if not (isinstance(n, int) and n < 1):
                        pe.wait_ge(scores_read, n)
                    for s in range(2):
                        for c in range(CC):
                            mm = pe.matmul(ps_score[s][:, :], xnT[:, c, :], keymap[:, c, s * 512:(s + 1) * 512],
                                           start=(c == 0), stop=(c == CC - 1))
                    mm.then_inc(score_mm, 1)

                def step(n, par):
                    for h in range(NH):
                        if h == 1 and not (isinstance(n, int) and n == TILES - 1):
                            route(n + 1, 1 - par)
                        pe.wait_ge(diag_ready, n * NH + (h + 1))
                        if h == 0 and not (isinstance(n, int) and n < 2):
                            pe.wait_ge(sum3_done, n - 1)
                        for k in range(K):
                            mm = pe.matmul(ps_out[par], diag[:, h % 2, k, :], rows[:, h % SLOTS, k, C:W2],
                                           start=(h == 0 and k == 0), stop=(h == NH - 1 and k == K - 1))
                        mm.then_inc(chunk_done, 1)
                route(0, 0)
                tiles(pe, step)

            @block.scalar
            def _(act):
                def route(n, par):
                    act.wait_ge(x2_in[par], 8 * (n - par) + 16)
                    if not (isinstance(n, int) and n < 2):
                        act.wait_ge(hid_ready, NH * (n - 1))
                    act.activation(ps_x2[par], x2_sb[:, par], ACT.Copy).then_inc(x2c_ready, 1)
                    act.wait_ge(xT_mm, n + 1)
                    if not (isinstance(n, int) and n < 1):
                        act.wait_ge(score_mm, n)
                    for c in range(CC):
                        last = act.activation(xnT[:, c, :], ps_xT[:, c, :], ACT.Identity, scale=bn_scale[:, c:c + 1],
                                              bias=bn_shift[:, c:c + 1])
                    last.then_inc(xn_ready, 1)

                def gates(n, par):
                    act.wait_ge(idx_ready, n + 1)
                    if not (isinstance(n, int) and n < 2):
                        act.wait_ge(coef_ready, NH * (n - 1))
                    act.activation(gate[:, par, :], sel[:, :, :].rearrange("p h k -> p (h k)"), ACT.Sigmoid)\
                        .then_inc(gate_ready, 1)

                def gelu(n, par, h):
                    act.wait_ge(hid_ready, n * NH + (h + 1))
                    act.activation(gel[:, par, h * K:(h + 1) * K], hid[:, par, h * K:(h + 1) * K], ACT.Gelu)\
                        .then_inc(gelu_ready, 1)

                def diags(n, par, h):
                    act.wait_ge(coef_ready, n * NH + (h + 1))
                    if not (isinstance(n, int) and n * NH + h < 2):
                        act.wait_ge(chunk_done, n * NH + (h - 1))
                    for k in range(K):
                        last = act.activation(diag[:, h % 2, k, :], ident[:, :], ACT.Copy,
                                              scale=coef[:, par, h * K + k:h * K + k + 1])
                    last.then_inc(diag_ready, 1)

                def std(n, par):
                    act.wait_ge(var3_ready, n + 1)
                    act.activation(sd3[:, :], mv3[:, 1:2], ACT.Sqrt, bias=eps_col[:, :]).then_inc(std3_ready, 1)
                act.wait_ge(norm_ready, 1)
                route(0, 0)
                gates(0, 0)

                def step(n, par):
                    more = not (isinstance(n, int) and n == TILES - 1)
                    for h in range(NH):
                        gelu(n, par, h)
                        diags(n, par, h)
                        if h == 1:
                            if not (isinstance(n, int) and n < 1):
                                std(n - 1, 1 - par)
                            if more:
                                route(n + 1, 1 - par)
                        if h == ROUTE_AT and more:
                            gates(n + 1, 1 - par)
                tiles(act, step)
                std(TILES - 1, 1)

            @block.vector
            def _(dve):
                def route(n, par):
                    dve.wait_ge(score_mm, n + 1)
                    if not (isinstance(n, int) and n < 1):
                        dve.wait_ge(gate_ready, n)
                    rest(dve, dve_rests)
                    def score(p, h):
                        return ps_score[p][:, h * NK:(h + 1) * NK]
                    for p in range(2):
                        for h in range(NH):
                            dve.max(out=top[:, p, h, :], in_=score(p, h))
                    dve.drain()
                    for p in range(2):
                        for h in range(NH):
                            last = dve.max_index(out=top_i[:, p, h, :], in_max=top[:, p, h, :], in_values=score(p, h))
                    last.then_inc(scores_read, 1)
                    dve.tensor_tensor(pair[:, :, :, :], top[:, 0, :, :, None].to_broadcast([P, NH, K, K]),
                                      top[:, 1, :, None, :].to_broadcast([P, NH, K, K]), ALU.add)
                    dve.drain()
                    for h in range(NH):
                        dve.max(out=sel[:, h, :], in_=pair[:, h, :, :].rearrange("p a b -> p (a b)"))
                    dve.drain()
                    for h in range(NH):
                        dve.max_index(out=sel_i[:, h, :], in_max=sel[:, h, :],
                                      in_values=pair[:, h, :, :].rearrange("p a b -> p (a b)"))
                    dve.drain()
                    flat_i = sel_i[:, :, :].rearrange("p h k -> p (h k)")
                    dve.tensor_scalar(half_i[:, 0, :], flat_i, 3, None, ALU.logical_shift_right)
                    dve.tensor_scalar(half_i[:, 1, :], flat_i, K - 1, None, ALU.bitwise_and)
                    dve.drain()
                    for p in range(2):
                        dve.tensor_tensor(hot[:, p], half_i[:, p, :, None].to_broadcast([P, HK, K]),
                                          iota8[:, None, :].to_broadcast([P, HK, K]), ALU.is_equal)
                    dve.drain()
                    for p in range(2):
                        h4 = hot[:, p].rearrange("p (h k) j -> p h k j", h=NH)
                        dve.tensor_tensor(h4, h4, top_i[:, p, :, None, :].to_broadcast([P, NH, K, K]), ALU.mult)
                    dve.drain()
                    for p in range(2):
                        dve.tensor_reduce(half_key[:, p, :], hot[:, p], AX.X, ALU.add)
                    dve.drain()
                    dve.scalar_tensor_tensor(out=idx[:, par, :], in0=half_key[:, 0, :], scalar=float(NK),
                                             in1=half_key[:, 1, :], op0=ALU.mult, op1=ALU.add).then_inc(idx_ready, 1)

                def hidden(n, par, h):
                    dve.wait_ge(gathered[h % SLOTS], n * (2 * 16 * K) + 16 * K * (h // SLOTS + 1))
                    for k in range(K):
                        last = dve.tensor_tensor_reduce(
                            out=rows[:, h % SLOTS, k, 0:C], in0=rows[:, h % SLOTS, k, 0:C], in1=ps_x2[par], scale=1.0, scalar=0.0,
                            op0=ALU.mult, op1=ALU.add, accum_out=hid[:, par, h * K + k:h * K + k + 1])
                    last.then_inc(hid_ready, 1)

                def coefs(n, par, h):
                    dve.wait_ge(gelu_ready, n * NH + (h + 1))
                    s = slice(h * K, (h + 1) * K)
                    dve.tensor_tensor(coef[:, par, s], gel[:, par, s], gate[:, par, s], ALU.mult)\
                        .then_inc(coef_ready, 1)

                def norm(n, par):
                    dve.wait_ge(chunk_done, NH * (n + 1))
                    dve.tensor_tensor(y3[:, :], ps_out[par], x2_sb[:, par], ALU.add).then_inc(sum3_done, 1)
                    dve.drain()
                    dve.bn_stats(out=st3[:, :], in_=y3[:, :])
                    dve.drain()
                    dve.bn_aggr(out=mv3[:, :], in_=st3[:, :]).then_inc(var3_ready, 1)

                def scale(n, par):
                    dve.wait_ge(std3_ready, n + 1)
                    dve.reciprocal(rs3[:, :], sd3[:, :])
                    dve.drain()
                    if not (isinstance(n, int) and n < 2):
                        dve.wait_ge(y_out[par], 8 * (n - par))
                    dve.tensor_scalar(yo[:, par, :], y3[:, :], mv3[:, 0:1], rs3[:, :], ALU.subtract, ALU.mult)\
                        .then_inc(y_ready, 1)
                route(0, 0)

                def step(n, par):
                    old = not (isinstance(n, int) and n < 1)
                    more = not (isinstance(n, int) and n == TILES - 1)
                    dve.wait_ge(x2c_ready, n + 1)
                    dve.wait_ge(gate_ready, n + 1)
                    for h in range(NH):
                        hidden(n, par, h)
                        coefs(n, par, h)
                        if h == 0 and old:
                            norm(n - 1, 1 - par)
                        if h == 2 and old:
                            scale(n - 1, 1 - par)
                        if h == ROUTE_AT and more:
                            route(n + 1, 1 - par)
                tiles(dve, step)
                norm(TILES - 1, 1)
                scale(TILES - 1, 1)


def kernel(x, ctx_1024, L0_attn_qkv_w, L0_attn_qkv_b, L0_attn_proj_w, L0_attn_proj_b, L0_ffn_bn_gamma,
           L0_ffn_bn_beta, L0_ffn_w_q, L0_ffn_keys_p, L0_ffn_down, L0_ffn_up):
    import numpy as np
    import concourse.bacc as bacc
    from concourse import mybir
    from concourse.bass_utils import run_bass_kernel_spmd as run

    B, T, C = x.shape
    a = lambda v: np.ascontiguousarray(np.asarray(v))
    x, ctx_1024 = a(x), a(ctx_1024)
    hs = L0_attn_qkv_w.shape[0] // 3
    flat = x.reshape(B * T, C)
    kp = a(L0_ffn_keys_p)
    ins = {
        "x": flat,
        "xT": a(flat.T),
        "ctx_rows": ctx_1024,
        "ctx_cols": a(ctx_1024.transpose(2, 0, 1)),
        "wqkvT": a(a(L0_attn_qkv_w).T),
        "bqkv": a(L0_attn_qkv_b).reshape(3 * hs, 1),
        "projT": a(a(L0_attn_proj_w).reshape(C, C // hs, hs).transpose(2, 0, 1)).reshape(hs, C * (C // hs)),
        "projb": a(L0_attn_proj_b).reshape(1, C),
        "gamma": a(a(L0_ffn_bn_gamma).reshape(C // 128, 128).T),
        "beta": a(a(L0_ffn_bn_beta).reshape(C // 128, 128).T),
        "wq": a(L0_ffn_w_q),
        "keysT": a(kp.transpose(3, 2, 0, 1)).reshape(kp.shape[3], 2 * kp.shape[0], kp.shape[1]),
        "table": np.concatenate([a(L0_ffn_down), a(L0_ffn_up)], axis=1),
    }
    nc = bacc.Bacc("TRN2", target_bir_lowering=False, num_devices=1)
    arrays, args = {}, []
    for name, v in ins.items():
        arrays[f"in_{name}"] = v
        args.append(nc.dram_tensor(f"in_{name}", v.shape, mybir.dt.from_np(v.dtype), kind="ExternalInput").ap())
    args.append(nc.dram_tensor("out_y", (B * T, C), mybir.dt.float32, kind="ExternalOutput").ap())
    decoder_layer(nc, *args)
    r = run(nc, [arrays], core_ids=[0])
    return r.results[0]["out_y"].reshape(B, T, C)
```

```python
from contextlib import ExitStack

import concourse.bass as bass
from concourse import mybir

F32 = mybir.dt.float32
I32 = mybir.dt.int32
U32 = mybir.dt.uint32
ALU = mybir.AluOpType
ACT = mybir.ActivationFunctionType
AX = mybir.AxisListType

P = 128
BIG = 1e30
TINY = 1e-30
EPS = 1e-5


def decoder_layer(nc, x, xT, ctx_rows_d, ctx_cols_d, wqkvT_d, bqkv_d, projT_d, projb_d, gamma_d, beta_d, wq_d,
                  keysT_d, table_d, out_d):
    NB, S2, C = ctx_rows_d.shape
    T = x.shape[0] // NB
    NT = T // P
    CC = C // P
    HS = wqkvT_d.shape[1] // 3
    NHEAD = C // HS
    TILES = x.shape[0] // P
    KD, NPH, NK = keysT_d.shape
    NH = NPH // 2
    K = 8
    NE, W2 = table_d.shape
    NG = 4
    RG = (S2 + NG - 1) // NG
    RP = NG * RG
    W = T + 1
    SLOTS = 4
    assert NB == P // NG and C == T == 2 * P and W2 == 2 * C and NK == 64 and KD == P and NH == 2 * SLOTS

    ctx = ExitStack()
    with ctx:
        def sb(name, shape, dt=F32):
            return ctx.enter_context(nc.sbuf_tensor(name, shape, dt))

        def sem(name):
            return ctx.enter_context(nc.semaphore(name))

        x1_d = nc.dram_tensor("x1_scratch", (x.shape[0], C), F32, kind="Internal").ap()
        x2_d = nc.dram_tensor("x2_scratch", (x.shape[0], C), F32, kind="Internal").ap()
        dist_d = nc.dram_tensor("dist_scratch", (NB, RP * T), F32, kind="Internal").ap()

        bank = [ctx.enter_context(nc.psum_tensor(f"bank{i}", [P, 512], F32)) for i in range(8)]

        ident = sb("ident", [P, P])
        iota_i = sb("iota_i", [P, T], I32)
        iota = sb("iota", [P, T])
        iota8 = sb("iota8", [P, K])
        causal = sb("causal", [P, NT, P])
        ones = sb("ones", [P, RP])
        fold = sb("fold", [P, NB])
        GAP = 32
        wqkv = sb("wqkv", [P, CC, 2 * GAP + HS])
        bias = sb("bias", [2 * GAP + HS, 1])
        proj = sb("proj", [HS + 1, C])
        gamma = sb("gamma", [P, CC])
        beta = sb("beta", [P, CC])
        keymap = sb("keymap", [P, CC, NPH * NK])
        ctx_rows = sb("ctx_rows", [S2, NB, C])
        ctx_norm = sb("ctx_norm", [RP, NB])
        bn = sb("bn", [P, CC, NB, 6])
        bn_mv = sb("bn_mv", [P, CC, 2])
        bn_scale = sb("bn_scale", [P, CC])
        bn_shift = sb("bn_shift", [P, CC])
        bn_tmp = sb("bn_tmp", [P, CC])
        eps_col = sb("eps_col", [P, 1])

        x2_tile = sb("x2_tile", [P, 2, C])

        w_in = sem("w_in")
        wq_in = sem("wq_in")
        ctx_in = [sem(f"ctx_in{i}") for i in range(NB // 8)]
        consts = sem("consts")
        setup_v = sem("setup_v")
        keymap_mm = sem("keymap_mm")
        keymap_done = sem("keymap_done")
        x_in = [sem(f"x_in{i}") for i in range(2)]
        p_in = sem("p_in")
        xT_in = [sem(f"xT_in{i}") for i in range(2)]
        qkv_mm = sem("qkv_mm")
        qk_ready = sem("qk_ready")
        vT_ready = sem("vT_ready")
        v_mm = sem("v_mm")
        v_ready = sem("v_ready")
        wei_mm = sem("wei_mm")
        weid_ready = sem("weid_ready")
        weio_ready = sem("weio_ready")
        head_mm = sem("head_mm")
        head_ready = sem("head_ready")
        attn_mm = sem("attn_mm")
        sum_done = sem("sum_done")
        var_ready = sem("var_ready")
        std_ready = sem("std_ready")
        x1_ready = sem("x1_ready")
        x1_out = [sem(f"x1_out{i}") for i in range(2)]
        x1T_mm = sem("x1T_mm")
        x1T_ready = sem("x1T_ready")
        ctxm2_ready = sem("ctxm2_ready")
        sq_ready = sem("sq_ready")
        dist_mm = sem("dist_mm")
        dist_ready = sem("dist_ready")
        root_ready = sem("root_ready")
        dist_out = [sem(f"dist_out{i}") for i in range(2)]
        cost_in = [sem(f"cost_in{g}") for g in range(NG)]
        table_init = sem("table_init")
        path_done = sem("path_done")
        bounds_mm = sem("bounds_mm")
        bounds_ready = sem("bounds_ready")
        x1_in = [sem(f"x1_in{i}") for i in range(2)]
        ramp_ready = sem("ramp_ready")
        mask_ready = sem("mask_ready")
        warp_mm = sem("warp_mm")
        sum2_done = sem("sum2_done")
        shift2_ready = sem("shift2_ready")
        var2_ready = sem("var2_ready")
        std2_ready = sem("std2_ready")
        x2_ready = sem("x2_ready")
        x2_out = [sem(f"x2_out{i}") for i in range(2)]
        x2T_mm = sem("x2T_mm")
        bn_done = sem("bn_done")
        bnvar_ready = sem("bnvar_ready")
        bnstd_ready = sem("bnstd_ready")
        norm_ready = sem("norm_ready")
        pool_rests, dve_rests, act_rests = sem("pool_rests"), sem("dve_rests"), sem("act_rests")
        x2_in = [sem(f"x2_in{i}") for i in range(2)]
        x2c_ready = sem("x2c_ready")
        xT_mm = sem("xT_mm")
        xn_ready = sem("xn_ready")
        score_mm = sem("score_mm")
        scores_read = sem("scores_read")
        idx_ready = sem("idx_ready")
        gate_ready = sem("gate_ready")
        gathered = [[sem(f"gathered{i}{half}") for half in "ab"] for i in range(SLOTS)]
        hid_ready = sem("hid_ready")
        gelu_ready = sem("gelu_ready")
        coef_ready = sem("coef_ready")
        diag_ready = sem("diag_ready")
        chunk_done = sem("chunk_done")
        sum3_done = sem("sum3_done")
        var3_ready = sem("var3_ready")
        std3_ready = sem("std3_ready")
        y_ready = sem("y_ready")
        y_out = [sem(f"y_out{i}") for i in range(2)]

        def rest(eng, spare):
            eng.sem_inc(spare, 1)

        def later(b, n):
            return not (isinstance(b, int) and b < n)

        def pipeline(eng, stages, peel, unroll=2, total=NB):
            def step(i, par):
                for stage, lag in stages:
                    if lag is None:
                        stage()
                        continue
                    b = i - lag
                    if not isinstance(b, int) or 0 <= b < total:
                        stage(b, (par + lag) % 2)
            for i in range(peel):
                step(i, i % 2)
            with eng.Fori(0, (total - peel) // unroll) as j:
                for u in range(unroll):
                    step(j * unroll + (peel + u), (peel + u) % 2)
            for i in range(total, total + max(lag or 0 for _, lag in stages)):
                step(i, i % 2)

        def dmas(b, par):
            return 8 * (b - par) + 16

        with ExitStack() as st:
            def sa(name, shape, dt=F32):
                return st.enter_context(nc.sbuf_tensor(name, shape, dt))

            projT = sa("projT", [HS, C * NHEAD])
            ctx_cols = sa("ctx_cols", [P, CC, NB, S2])
            ctxm2 = sa("ctxm2", [P, 2, CC, RP])
            x_sb = sa("x_sb", [P, 2, NT, C])
            xT_sb = sa("xT_sb", [P, 2, CC, T])
            qT = sa("qT", [HS, 2, T])
            kT = sa("kT", [HS, 2, T])
            vT = sa("vT", [HS, 2, T])
            v_sb = sa("v_sb", [P, 2, NT, HS])
            weiT = sa("weiT", [P, 2, 3, P])
            headT = sa("headT", [HS + 1, 2, T])
            y1 = sa("y1", [P, 2, NT, C])
            st1 = sa("st1", [P, 2, NT, 6])
            mv1 = sa("mv1", [P, 2, NT, 2])
            sd1 = sa("sd1", [P, 2, NT])
            rs1 = sa("rs1", [P, 2, NT])
            x1_sb = sa("x1_sb", [P, 2, NT, C])
            x1T = sa("x1T", [P, 2, CC, T])
            x1sq = sa("x1sq", [P, CC, T])
            x1sum = sa("x1sum", [P, 2, T])
            dist_sb = sa("dist_sb", [RP, 2, T])
            sq_scr = sa("sq_scr", [S2, 8, C])

            ps_qkv, ps_v = bank[0][0:2 * GAP + HS, 0:T], bank[6][:, 0:NT * HS].rearrange("p (t d) -> p t d", t=NT)
            ps_wei = bank[1][:, 0:3 * P].rearrange("p (k t) -> p k t", k=3)
            ps_head = bank[2][0:HS, 0:T]
            ps_attn = bank[3][:, :].rearrange("p (t c) -> p t c", t=NT)
            ps_x1T = bank[4][:, :].rearrange("p (c t) -> p c t", c=CC)
            ps_dist = bank[5][0:RP, 0:T]

            block = st.enter_context(nc.Block())
            xb = x.rearrange("(b t p) c -> b p t c", b=NB, t=NT)
            x1b = x1_d.rearrange("(b t p) c -> b p t c", b=NB, t=NT)
            xTb = xT.rearrange("(k p) (b t) -> b p k t", k=CC, b=NB)

            @block.sync
            def _(sp):
                def one(ap, b):
                    return ap[bass.ds(b, 1)].rearrange("a p t c -> (a p) t c")

                def load_xT(b, par):
                    if isinstance(b, int) and b == 1:
                        for dst, src in ((projT[:, :], projT_d), (proj[HS:HS + 1, :], projb_d),
                                         (gamma[:, :], gamma_d), (beta[:, :], beta_d)):
                            sp.dma_start(dst, src).then_inc(p_in, 16)
                    if isinstance(b, int) and 2 <= b < 2 + NB // 8:
                        some = slice(8 * (b - 2), 8 * (b - 1))
                        sp.dma_start(ctx_rows[:, some, :], ctx_rows_d[some].rearrange("b s c -> s b c"))\
                            .then_inc(ctx_in[b - 2], 16)
                        sp.dma_start(ctx_cols[:, :, some, :],
                                     ctx_cols_d[:, some].rearrange("(k p) b s -> p k b s", k=CC))\
                            .then_inc(ctx_in[b - 2], 16)
                    if later(b, 2):
                        sp.wait_ge(qkv_mm, b - 1)
                    sp.dma_start(xT_sb[:, par], one(xTb, b)).then_inc(xT_in[par], 16)

                def load_x(b, par):
                    if later(b, 2):
                        sp.wait_ge(sum_done, b - 1)
                    sp.dma_start(x_sb[:, par], one(xb, b)).then_inc(x_in[par], 16)

                def store_x1(b, par):
                    sp.wait_ge(x1_ready, b + 1)
                    sp.dma_start(one(x1b, b), x1_sb[:, par]).then_inc(x1_out[par], 16)

                def store_dist(b, par):
                    sp.wait_ge(root_ready, b + 1)
                    sp.dma_start(dist_d[bass.ds(b, 1)].rearrange("a (i j) -> (a i) j", i=RP),
                                 dist_sb[:, par]).then_inc(dist_out[par], 16)

                for part in range(3):
                    of = slice(HS * part, HS * (part + 1))
                    at = slice(GAP * part, GAP * part + HS)
                    sp.dma_start(wqkv[:, :, at], wqkvT_d[:, of].rearrange("(k p) d -> p k d", k=CC)).then_inc(w_in, 16)
                    sp.dma_start(bias[at, :], bqkv_d[of]).then_inc(w_in, 16)
                pipeline(sp, [(load_xT, 0), (load_x, 5), (store_x1, 7), (store_dist, 10)], 12)
                for par in range(2):
                    sp.wait_ge(x1_out[par], 16 * NB // 2)
                    sp.wait_ge(dist_out[par], 16 * NB // 2)

            @block.gpsimd
            def _(pool):
                pool.memset(wqkv[:, :, HS:GAP], 0.0)
                pool.memset(wqkv[:, :, GAP + HS:2 * GAP], 0.0)
                pool.memset(ones[:, :], 1.0)
                pool.memset(headT[:, :, :], 1.0)
                pool.memset(ctxm2[:, :, :, :], 0.0)
                pool.memset(ctx_norm[:, :], 0.0)
                pool.memset(eps_col[:, :], EPS)
                pool.memset(ident[:, :], 0.0)
                pool.memset(causal[:, :, :], 1.0)
                pool.iota(iota_i[:, :], [[1, T]], base=0, channel_multiplier=0)
                pool.drain()
                pool.affine_select(out=ident[:, :], in_=ident[:, :], compare_op=ALU.not_equal, fill=1.0, base=0,
                                   pattern=[[-1, P]], channel_multiplier=1)
                pool.affine_select(out=causal[:, :, :], in_=causal[:, :, :], compare_op=ALU.is_ge, fill=0.0,
                                   base=0, pattern=[[0, NT], [1, P]], channel_multiplier=-1)
                pool.drain()
                pool.nop().then_inc(consts, 1)

                def squares(b, par):
                    pool.wait_ge(x1T_ready, b + 1)
                    pool.tensor_tensor(x1sq[:, :, :], x1T[:, par], x1T[:, par], ALU.mult)
                    pool.drain()
                    if later(b, 2):
                        pool.wait_ge(dist_mm, b - 1)
                    pool.tensor_tensor(x1sum[:, par, :], x1sq[:, 0, :], x1sq[:, 1, :], ALU.add).then_inc(sq_ready, 1)
                    pool.drain()
                pipeline(pool, [(squares, 0)], 2)

            @block.tensor
            def _(pe):
                def qkv(b, par):
                    pe.wait_ge(xT_in[par], dmas(b, par))
                    if later(b, 1):
                        pe.wait_ge(vT_ready, b)
                    for c in range(CC):
                        mm = pe.matmul(ps_qkv, wqkv[:, c, :], xT_sb[:, par, c, :], start=(c == 0), stop=(c == CC - 1))
                    mm.then_inc(qkv_mm, 1)

                def turn_v(b, par):
                    pe.wait_ge(vT_ready, b + 1)
                    if later(b, 1):
                        pe.wait_ge(v_ready, b)
                    for t in range(NT):
                        mm = pe.matmul(ps_v[:, t, :], vT[:, par, t * P:(t + 1) * P], ident[0:HS, 0:HS],
                                       start=True, stop=True)
                    mm.then_inc(v_mm, 1)

                def wei(b, par):
                    pe.wait_ge(qk_ready, b + 1)
                    if later(b, 1):
                        pe.wait_ge(weio_ready, b)
                    pe.matmul(ps_wei[:, 0, :], kT[:, par, P:T], qT[:, par, P:T], start=True, stop=True)
                    pe.matmul(ps_wei[:, 1:3, :].rearrange("p k t -> p (k t)"), kT[:, par, 0:P], qT[:, par, :],
                              start=True, stop=True).then_inc(wei_mm, 1)

                def head(b, par):
                    pe.wait_ge(v_ready, b + 1)
                    pe.wait_ge(weid_ready, b + 1)
                    pe.wait_ge(weio_ready, b + 1)
                    if later(b, 1):
                        pe.wait_ge(head_ready, b)
                    pe.matmul(ps_head, v_sb[:, par, 0, :], weiT[:, par, 1:3, :].rearrange("p k t -> p (k t)"),
                              start=True, stop=False)
                    pe.matmul(ps_head[:, P:T], v_sb[:, par, 1, :], weiT[:, par, 0, :], start=False, stop=True)\
                        .then_inc(head_mm, 1)

                def attn(b, par):
                    pe.wait_ge(head_ready, b + 1)
                    if not later(b, 1):
                        pe.wait_ge(setup_v, 1)
                    if later(b, 1):
                        pe.wait_ge(sum_done, b)
                    for t in range(NT):
                        mm = pe.matmul(ps_attn[:, t, :], headT[:, par, t * P:(t + 1) * P], proj[:, :],
                                       start=True, stop=True)
                    mm.then_inc(attn_mm, 1)

                def turn_x1(b, par):
                    pe.wait_ge(x1_ready, b + 1)
                    if later(b, 1):
                        pe.wait_ge(x1T_ready, b)
                    for c in range(CC):
                        for t in range(NT):
                            mm = pe.transpose(ps_x1T[:, c, t * P:(t + 1) * P], x1_sb[:, par, t, c * P:(c + 1) * P],
                                              ident[:, :])
                    mm.then_inc(x1T_mm, 1)

                def dist(b, par):
                    pe.wait_ge(ctxm2_ready, b + 1)
                    pe.wait_ge(x1T_ready, b + 1)
                    if later(b, 1):
                        pe.wait_ge(dist_ready, b)
                    for c in range(CC):
                        pe.matmul(ps_dist, ctxm2[:, par, c, :], x1T[:, par, c, :], start=(c == 0), stop=False)
                    pe.wait_ge(sq_ready, b + 1)
                    pe.matmul(ps_dist, ones[:, :], x1sum[:, par, :], start=False, stop=True).then_inc(dist_mm, 1)

                pe.wait_ge(consts, 1)
                pe.wait_ge(w_in, 16 * 6)
                pipeline(pe, [(head, 2), (qkv, 0), (wei, 1), (turn_v, 1), (attn, 3), (turn_x1, 6), (dist, 7)], 10)

            @block.scalar
            def _(act):
                def qkv(b, par):
                    act.wait_ge(qkv_mm, b + 1)
                    if later(b, 2):
                        act.wait_ge(wei_mm, b - 1)
                    act.activation(qT[:, par, :], ps_qkv[0:HS, :], ACT.Identity, bias=bias[0:HS, :])
                    act.activation(kT[:, par, :], ps_qkv[GAP:GAP + HS, :], ACT.Identity, bias=bias[GAP:GAP + HS, :])\
                        .then_inc(qk_ready, 1)
                    if later(b, 2):
                        act.wait_ge(v_mm, b - 1)
                    act.activation(vT[:, par, :], ps_qkv[2 * GAP:, :], ACT.Identity, bias=bias[2 * GAP:, :])\
                        .then_inc(vT_ready, 1)

                def wei_off(b, par):
                    act.wait_ge(weid_ready, b + 1)
                    act.wait_ge(wei_mm, b + 1)
                    if later(b, 2):
                        act.wait_ge(head_mm, b - 1)
                    act.activation(weiT[:, par, 2, :], ps_wei[:, 2, :], ACT.Copy).then_inc(weio_ready, 1)

                def x1_cols(b, par):
                    act.wait_ge(x1T_mm, b + 1)
                    if later(b, 2):
                        act.wait_ge(dist_mm, b - 1)
                        act.wait_ge(sq_ready, b - 1)
                    act.activation(x1T[:, par], ps_x1T[:, :, :], ACT.Copy).then_inc(x1T_ready, 1)

                def ctx_scale(b, par):
                    if not later(b, 1):
                        for part in ctx_in:
                            act.wait_ge(part, 32)
                    if later(b, 2):
                        act.wait_ge(dist_mm, b - 1)
                    rest(act, act_rests)
                    act.activation(ctxm2[:, par, :, 0:S2],
                                   ctx_cols[:, :, bass.ds(b, 1), :].rearrange("p k a s -> p k (a s)"),
                                   ACT.Copy, scale=-2.0).then_inc(ctxm2_ready, 1)

                def head(b, par):
                    act.wait_ge(head_mm, b + 1)
                    if later(b, 2):
                        act.wait_ge(attn_mm, b - 1)
                    act.activation(headT[0:HS, par, :], ps_head, ACT.Copy).then_inc(head_ready, 1)

                def std(b, par):
                    act.wait_ge(var_ready, b + 1)
                    act.activation(sd1[:, par, :], mv1[:, par, :, 1], ACT.Sqrt, bias=eps_col[:, :])\
                        .then_inc(std_ready, 1)

                def root(b, par):
                    act.wait_ge(dist_ready, b + 1)
                    act.activation(dist_sb[:, par, :], dist_sb[:, par, :], ACT.Sqrt).then_inc(root_ready, 1)

                act.wait_ge(consts, 1)
                act.wait_ge(w_in, 16 * 6)
                pipeline(act, [(root, 9), (head, 2), (qkv, 0), (wei_off, 1), (ctx_scale, 6), (x1_cols, 6), (std, 4)], 12)

            @block.vector
            def _(dve):
                def v(b, par):
                    dve.wait_ge(v_mm, b + 1)
                    if later(b, 2):
                        dve.wait_ge(head_mm, b - 1)
                    dve.tensor_copy(v_sb[:, par], ps_v).then_inc(v_ready, 1)

                def wei_diag(b, par):
                    dve.wait_ge(wei_mm, b + 1)
                    if later(b, 2):
                        dve.wait_ge(head_mm, b - 1)
                    dve.tensor_tensor(weiT[:, par, 0:2, :], ps_wei[:, 0:2, :], causal[:, :, :], ALU.mult)\
                        .then_inc(weid_ready, 1)

                def dist(b, par):
                    dve.wait_ge(dist_mm, b + 1)
                    if later(b, 2):
                        dve.wait_ge(dist_out[par], dmas(b, par) - 16)
                    dve.tensor_scalar(dist_sb[:, par, :], ps_dist, ctx_norm[:, bass.ds(b, 1)], TINY, ALU.add, ALU.max)\
                        .then_inc(dist_ready, 1)

                def residual(b, par):
                    dve.wait_ge(attn_mm, b + 1)
                    dve.wait_ge(x_in[par], dmas(b, par))
                    dve.tensor_tensor(y1[:, par], ps_attn, x_sb[:, par], ALU.add).then_inc(sum_done, 1)

                def recip(b, par):
                    dve.wait_ge(std_ready, b + 1)
                    dve.reciprocal(rs1[:, par, :], sd1[:, par, :])

                def settle():
                    dve.drain()

                def stats(b, par):
                    for t in range(NT):
                        dve.bn_stats(out=st1[:, par, t, :], in_=y1[:, par, t, :])

                def aggr(b, par):
                    for t in range(NT):
                        last = dve.bn_aggr(out=mv1[:, par, t, :], in_=st1[:, par, t, :])
                    last.then_inc(var_ready, 1)

                def scale(b, par):
                    if later(b, 2):
                        dve.wait_ge(x1_out[par], dmas(b, par) - 16)
                        dve.wait_ge(x1T_mm, b - 1)
                    for t in range(NT):
                        last = dve.tensor_scalar(x1_sb[:, par, t, :], y1[:, par, t, :], mv1[:, par, t, 0:1],
                                                 rs1[:, par, t:t + 1], ALU.subtract, ALU.mult)
                    last.then_inc(x1_ready, 1)

                def norms(b, par):
                    if isinstance(b, int) and b < NB // 8:
                        dve.wait_ge(ctx_in[b], 32)
                        for k in range(8 * b, 8 * b + 8):
                            dve.tensor_tensor_reduce(out=sq_scr[:, k % 8, :], in0=ctx_rows[:, k, :],
                                                     in1=ctx_rows[:, k, :], scale=1.0, scalar=0.0, op0=ALU.mult,
                                                     op1=ALU.add, accum_out=ctx_norm[0:S2, k:k + 1])

                def setup(b, par):
                    if not later(b, 1):
                        dve.wait_ge(p_in, 64)
                        dve.tensor_reduce(proj[0:HS, :], projT[:, :].rearrange("d (c h) -> d c h", h=NHEAD), AX.X,
                                          ALU.add).then_inc(setup_v, 1)
                        dve.tensor_copy(iota[:, :], iota_i[:, :])
                        dve.tensor_copy(iota8[:, :], iota_i[:, 0:K])
                        dve.tensor_reduce(fold[:, :], ident[:, :].rearrange("p (g b) -> p b g", g=NG), AX.X, ALU.add)

                dve.wait_ge(consts, 1)
                pipeline(dve, [(residual, 4), (recip, 5), (dist, 8), (wei_diag, 1), (v, 1), (setup, 1), (settle, None),
                               (norms, 4), (stats, 4), (scale, 5), (settle, None), (aggr, 4)], 10)

        with ExitStack() as st:
            def sw(name, shape, dt=F32):
                return st.enter_context(nc.sbuf_tensor(name, shape, dt))

            cost = sw("cost", [P, RG * T])
            acc = sw("acc", [P, (RG + 1) * W])
            best = sw("best", [P, RG * T])
            is_left = sw("is_left", [P, RG * T])
            entry = sw("entry", [P, RG * T])
            picked = sw("picked", [P, 2, T])
            path = sw("path", [P, RG + 1])
            lo_hi = sw("lo_hi", [P, 2, RP])
            bounds = sw("bounds", [RP, 2, NB])
            wq_rows = sw("wq_rows", [P, NPH, C])
            keysT = sw("keysT", [P, NPH, NK])
            ramp = sw("ramp", [S2, 2, T])
            mask = sw("mask", [S2, 2, T])
            x1_sb = sw("x1_again", [P, 2, NT, C])
            y2 = sw("y2", [P, 2, NT, C])
            st2 = sw("st2", [P, 2, NT, 6])
            mv2 = sw("mv2", [P, 2, NT, 2])
            sd2 = sw("sd2", [P, 2, NT])
            rs2 = sw("rs2", [P, 2, NT])
            nb2 = sw("nb2", [P, 2, NT])
            x2_sb = sw("x2_sb", [P, 2, NT, C])
            ps_bounds = bank[0][0:RP, 0:2 * NB].rearrange("p (a b) -> p a b", a=2)
            ps_warp = [bank[1 + i][:, :].rearrange("p (t c) -> p t c", t=NT) for i in range(2)]
            ps_x2T = [bank[3 + i][:, :].rearrange("p (c t) -> p c t", c=CC) for i in range(2)]
            ps_key = [bank[4 + i] for i in range(4)]
            x1b = x1_d.rearrange("(b t p) c -> b p t c", b=NB, t=NT)
            x2b = x2_d.rearrange("(b t p) c -> b p t c", b=NB, t=NT)
            acc3 = acc[:, :].rearrange("p (r w) -> p r w", w=W)

            block = st.enter_context(nc.Block())

            @block.sync
            def _(sp):
                for g in range(NG):
                    sp.dma_start(cost[NB * g:NB * (g + 1), :], dist_d[:, RG * T * g:RG * T * (g + 1)])\
                        .then_inc(cost_in[g], 16)
                sp.dma_start(keysT[:, :, :], keysT_d).then_inc(wq_in, 16)
                sp.dma_start(wq_rows[:, :, :], wq_d.rearrange("(g d) c -> d g c", g=NPH)).then_inc(wq_in, 16)

                def one(ap, b):
                    return ap[bass.ds(b, 1)].rearrange("a p t c -> (a p) t c")

                def load(b, par):
                    if later(b, 2):
                        sp.wait_ge(sum2_done, b - 1)
                    sp.dma_start(x1_sb[:, par], one(x1b, b)).then_inc(x1_in[par], 16)

                def store(b, par):
                    sp.wait_ge(x2_ready, b + 1)
                    sp.dma_start(one(x2b, b), x2_sb[:, par]).then_inc(x2_out[par], 16)

                pipeline(sp, [(load, 0), (store, 3)], 6)
                for n in range(2):
                    sp.dma_start(x2_tile[:, n], x2_d[n * P:(n + 1) * P]).then_inc(x2_in[n], 16)
                for par in range(2):
                    sp.wait_ge(x2_out[par], 16 * NB // 2)

            @block.gpsimd
            def _(pool):
                pool.memset(acc3[:, :, 0:1], BIG)
                pool.memset(acc[0:NB, 1:W], BIG)
                pool.drain()
                pool.memset(acc[0:NB, 0:1], 0.0)
                pool.drain()
                short = S2 - RG * (NG - 1)
                pool.memset(acc3[P - NB:P, short + 1:, 1:W], BIG)
                pool.memset(best[P - NB:P, short * T:], BIG)
                pool.drain()
                pool.memset(lo_hi[:, :, :], 0.0)
                pool.memset(path[:, :], 0.0)
                pool.drain()
                pool.nop().then_inc(table_init, 1)

            @block.scalar
            def _(act):
                act.wait_ge(keymap_mm, 1)
                for i in range(4):
                    kc = act.activation(keymap[:, i // 2, (i % 2) * 512:(i % 2 + 1) * 512], ps_key[i][:, :], ACT.Copy)
                kc.then_inc(keymap_done, 1)
                act.wait_ge(bounds_mm, 1)
                act.activation(bounds[:, 0, :], ps_bounds[:, 0, :], ACT.Identity, scale=-4.0, bias=ones[0:RP, 0:1])
                act.activation(bounds[:, 1, :], ps_bounds[:, 1, :], ACT.Copy).then_inc(bounds_ready, 1)
                act.wait_ge(bounds_ready, 1)

                def ramps(b, par):
                    if later(b, 2):
                        act.wait_ge(mask_ready, b - 1)
                    rest(act, act_rests)
                    act.activation(ramp[:, par, :], iota[0:S2, :], ACT.Relu, scale=4.0,
                                   bias=bounds[0:S2, 0, bass.ds(b, 1)]).then_inc(ramp_ready, 1)

                def std(b, par):
                    act.wait_ge(var2_ready, b + 1)
                    act.activation(sd2[:, par, :], mv2[:, par, :, 1], ACT.Sqrt, bias=eps_col[:, :])\
                        .then_inc(std2_ready, 1)

                def norm(b, par):
                    act.wait_ge(shift2_ready, b + 1)
                    if later(b, 2):
                        act.wait_ge(x2_out[par], dmas(b, par) - 16)
                        act.wait_ge(x2T_mm, b - 1)
                    for t in range(NT):
                        last = act.activation(x2_sb[:, par, t, :], y2[:, par, t, :], ACT.Identity,
                                              scale=rs2[:, par, t:t + 1], bias=nb2[:, par, t:t + 1])
                    last.then_inc(x2_ready, 1)
                pipeline(act, [(norm, 4), (ramps, 0), (std, 3)], 6)
                act.wait_ge(bnvar_ready, 1)
                act.activation(bn_tmp[:, :], bn_mv[:, :, 1], ACT.Sqrt, bias=eps_col[:, :]).then_inc(bnstd_ready, 1)

            @block.tensor
            def _(pe):
                pe.wait_ge(wq_in, 32)
                for c in range(CC):
                    for g in range(NPH):
                        mm = pe.matmul(ps_key[2 * c + g // NH][:, (g % NH) * NK:(g % NH + 1) * NK],
                                       wq_rows[:, g, c * P:(c + 1) * P], keysT[:, g, :], start=True, stop=True)
                mm.then_inc(keymap_mm, 1)
                pe.wait_ge(path_done, 1)
                for a in range(2):
                    mm = pe.matmul(ps_bounds[:, a, :], lo_hi[:, a, :], fold[:, :], start=True, stop=True)
                mm.then_inc(bounds_mm, 1)

                def warp(b, par):
                    pe.wait_ge(mask_ready, b + 1)
                    if later(b, 2):
                        pe.wait_ge(sum2_done, b - 1)
                    for t in range(NT):
                        mm = pe.matmul(ps_warp[par][:, t, :], mask[:, par, t * P:(t + 1) * P],
                                       ctx_rows[:, bass.ds(b, 1), :].rearrange("s a c -> s (a c)"),
                                       start=True, stop=True)
                    mm.then_inc(warp_mm, 1)

                def turn(b, par):
                    pe.wait_ge(x2_ready, b + 1)
                    if later(b, 2):
                        pe.wait_ge(bn_done, b - 1)
                    for c in range(CC):
                        for t in range(NT):
                            mm = pe.transpose(ps_x2T[par][:, c, t * P:(t + 1) * P],
                                              x2_sb[:, par, t, c * P:(c + 1) * P], ident[:, :])
                    mm.then_inc(x2T_mm, 1)
                pe.wait_ge(keymap_done, 1)
                pipeline(pe, [(turn, 4), (warp, 1)], 6)

            @block.vector
            def _(dve):
                dve.wait_ge(table_init, 1)
                for g in range(NG):
                    q = slice(NB * g, NB * (g + 1))
                    rows = min(RG, S2 - RG * g)
                    dve.wait_ge(cost_in[g], 16)
                    if g:
                        dve.tensor_copy(acc[q, 0:W], acc[NB * (g - 1):NB * g, RG * W:(RG + 1) * W])
                        dve.drain()

                    def row(w, t):
                        dve.tensor_tensor(best[q, bass.ds(t, T)], acc[q, bass.ds(w + 1, T)], acc[q, bass.ds(w, T)],
                                          ALU.min)
                        dve.drain()
                        dve.tensor_tensor_scan(acc[q, bass.ds(w + W + 1, T)], best[q, bass.ds(t, T)],
                                               cost[q, bass.ds(t, T)], BIG, ALU.min, ALU.add)
                        dve.drain()
                    U = 10
                    looped = rows // U * U if rows >= 2 * U else 0
                    if looped:
                        with dve.Fori(0, looped // U) as i:
                            w, t = i * (U * W), i * (U * T)
                            for u in range(U):
                                row(w + u * W, t + u * T)
                    for r in range(looped, rows):
                        row(r * W, r * T)

                best3 = best[:, :].rearrange("p (r t) -> p r t", t=T)
                left3 = is_left[:, :].rearrange("p (r t) -> p r t", t=T)
                entry3 = entry[:, :].rearrange("p (r t) -> p r t", t=T)
                dve.tensor_tensor(left3, acc3[:, 1:, 0:T], best3, ALU.is_lt)
                dve.tensor_tensor(entry3, acc3[:, 0:RG, 0:T], acc3[:, 0:RG, 1:W], ALU.is_le)
                dve.drain()
                dve.scalar_tensor_tensor(out=best3, in0=entry3, scalar=-0.75,
                                         in1=iota[:, None, :].to_broadcast([P, RG, T]), op0=ALU.mult, op1=ALU.add)
                dve.drain()
                dve.scalar_tensor_tensor(out=best[:, :], in0=is_left[:, :], scalar=-1.0, in1=best[:, :],
                                         op0=ALU.add, op1=ALU.mult)
                dve.drain()
                dve.tensor_tensor_scan(entry[:, :], is_left[:, :], best[:, :], 0.0, ALU.mult, ALU.subtract)

                dve.drain()
                dve.tensor_copy(best3[:, :, 0:1], entry3[:, :, 0:1])
                dve.tensor_tensor(best3[:, :, 1:T], entry3[:, :, 1:T], entry3[:, :, 0:T - 1], ALU.subtract)

                def climb(q, r, t, par):
                    dve.scalar_tensor_tensor(out=picked[q, par, :], in0=iota[q, :], scalar=path[q, bass.ds(r + 1, 1)],
                                             in1=best[q, bass.ds(t, T)], op0=ALU.is_le, op1=ALU.mult,
                                             accum_out=path[q, bass.ds(r, 1)])
                    dve.drain()
                for g in range(NG - 1, -1, -1):
                    q, rows = slice(NB * g, NB * (g + 1)), min(RG, S2 - RG * g)
                    if g == NG - 1:
                        dve.memset(path[q, rows:rows + 1], float(T - 1))
                    else:
                        dve.tensor_copy(path[q, RG:RG + 1], path[NB * (g + 1):NB * (g + 2), 0:1])
                    dve.drain()
                    U = 10
                    looped = rows // U * U if rows >= 2 * U else 0
                    if looped:
                        with dve.Fori(0, looped // U) as j:
                            r, t = j * -U, j * (-U * T)
                            for u in range(U):
                                climb(q, r + (rows - 1 - u), t + (rows - 1 - u) * T, u % 2)
                    for r in range(rows - looped - 1, -1, -1):
                        climb(q, r, r * T, r % 2)
                for g in range(NG):
                    q, rows = slice(NB * g, NB * (g + 1)), min(RG, S2 - RG * g)
                    for a in range(2):
                        dve.tensor_copy(lo_hi[q, a, RG * g:RG * g + rows], path[q, a:a + rows])
                dve.drain()
                dve.nop().then_inc(path_done, 1)
                dve.wait_ge(bounds_ready, 1)

                def masks(b, par):
                    dve.wait_ge(ramp_ready, b + 1)
                    if later(b, 2):
                        dve.wait_ge(warp_mm, b - 1)
                    dve.scalar_tensor_tensor(out=mask[:, par, :], in0=iota[0:S2, :],
                                             scalar=bounds[0:S2, 1, bass.ds(b, 1)], in1=ramp[:, par, :],
                                             op0=ALU.is_le, op1=ALU.min).then_inc(mask_ready, 1)

                def add(b, par):
                    dve.wait_ge(warp_mm, b + 1)
                    dve.wait_ge(x1_in[par], dmas(b, par))
                    if later(b, 2):
                        dve.wait_ge(x2_ready, b - 1)
                    dve.tensor_tensor(y2[:, par], ps_warp[par], x1_sb[:, par], ALU.add).then_inc(sum2_done, 1)

                def stats(b, par):
                    for t in range(NT):
                        dve.bn_stats(out=st2[:, par, t, :], in_=y2[:, par, t, :])

                def aggr(b, par):
                    for t in range(NT):
                        last = dve.bn_aggr(out=mv2[:, par, t, :], in_=st2[:, par, t, :])
                    last.then_inc(var2_ready, 1)

                def recip(b, par):
                    dve.wait_ge(std2_ready, b + 1)
                    dve.reciprocal(rs2[:, par, :], sd2[:, par, :])

                def shift(b, par):
                    dve.scalar_tensor_tensor(out=nb2[:, par, :], in0=mv2[:, par, :, 0], scalar=-1.0,
                                             in1=rs2[:, par, :], op0=ALU.mult, op1=ALU.mult)\
                        .then_inc(shift2_ready, 1)

                def chan_stats(b, par):
                    dve.wait_ge(x2T_mm, b + 1)
                    for c in range(CC):
                        last = dve.bn_stats(out=bn[:, c, bass.ds(b, 1), :].rearrange("p a s -> p (a s)"),
                                            in_=ps_x2T[par][:, c, :])
                    last.then_inc(bn_done, 1)

                def settle():
                    dve.drain()
                pipeline(dve, [(add, 2), (recip, 3), (settle, None), (masks, 0), (shift, 3), (chan_stats, 5),
                               (stats, 2), (settle, None), (aggr, 2)], 8, unroll=4)
                dve.drain()
                for c in range(CC):
                    last = dve.bn_aggr(out=bn_mv[:, c, :], in_=bn[:, c, :, :].rearrange("p b s -> p (b s)"))
                last.then_inc(bnvar_ready, 1)
                dve.wait_ge(bnstd_ready, 1)
                dve.reciprocal(bn_scale[:, :], bn_tmp[:, :])
                dve.drain()
                dve.tensor_tensor(bn_scale[:, :], bn_scale[:, :], gamma[:, :], ALU.mult)
                dve.drain()
                dve.tensor_tensor(bn_tmp[:, :], bn_mv[:, :, 0], bn_scale[:, :], ALU.mult)
                dve.drain()
                dve.tensor_tensor(bn_shift[:, :], beta[:, :], bn_tmp[:, :], ALU.subtract).then_inc(norm_ready, 1)

        with ExitStack() as st:
            def se(name, shape, dt=F32):
                return st.enter_context(nc.sbuf_tensor(name, shape, dt))

            HK = NH * K
            xnT = se("xnT", [P, CC, P])
            top = se("top", [P, 2, NH, K])
            top_i = se("top_i", [P, 2, NH, K], U32)
            pair = se("pair", [P, NH, K, K])
            sel = se("sel", [P, NH, K])
            sel_i = se("sel_i", [P, NH, K], U32)
            half_i = se("half_i", [P, 2, HK], U32)
            hot = se("hot", [P, 2, HK, K])
            half_key = se("half_key", [P, 2, HK])
            idx = se("idx", [P, 2, HK], U32)
            gate = se("gate", [P, 2, HK])
            rows = se("rows", [P, SLOTS, K, W2])
            hid = se("hid", [P, 2, HK])
            gel = se("gel", [P, 2, HK])
            coef = se("coef", [P, 2, HK])
            diag = se("diag", [P, 2, K, P])
            y3 = se("y3", [P, C])
            st3 = se("st3", [P, 6])
            mv3 = se("mv3", [P, 2])
            sd3 = se("sd3", [P, 1])
            rs3 = se("rs3", [P, 1])
            yo = se("yo", [P, 2, C])
            HALF = NH // 2 * NK
            ps_score = bank[0], bank[1]
            ps_xT = bank[2][:, 0:C].rearrange("p (c t) -> p c t", c=CC)
            ps_x2 = [bank[3][:, 0:C], bank[4][:, 0:C]]
            ps_out = [bank[5][:, 0:C], bank[6][:, 0:C]]
            x2t = x2_d.rearrange("(n p) c -> n p c", p=P)
            outt = out_d.rearrange("(n p) c -> n p c", p=P)
            ROUTE_AT = 3

            def tiles(eng, step):
                for n in range(2):
                    step(n, n)
                with eng.Fori(1, TILES // 2 - 1) as j:
                    for par in range(2):
                        step(2 * j + par, par)
                for n in range(TILES - 2, TILES):
                    step(n, n % 2)

            block = st.enter_context(nc.Block())

            @block.sync
            def _(sp):
                def load(n, par):
                    sp.wait_ge(sum3_done, n - 1)
                    sp.wait_ge(xT_mm, n - 1)
                    sp.wait_ge(x2c_ready, n - 1)
                    sp.dma_start(x2_tile[:, par], x2t[bass.ds(n, 1)].rearrange("a p c -> (a p) c"))\
                        .then_inc(x2_in[par], 16)

                def store(n, par):
                    sp.wait_ge(y_ready, n + 1)
                    sp.dma_start(outt[bass.ds(n, 1)].rearrange("a p c -> (a p) c"), yo[:, par])\
                        .then_inc(y_out[par], 16)
                def step(n, par):
                    if later(n, 1) and not (isinstance(n, int) and n == TILES - 1):
                        load(n + 1, 1 - par)
                    if not (isinstance(n, int) and n < 1):
                        store(n - 1, 1 - par)
                tiles(sp, step)
                store(TILES - 1, 1)
                for par in range(2):
                    sp.wait_ge(y_out[par], 16 * TILES // 2)

            @block.gpsimd
            def _(pool):
                def step(n, par):
                    pool.wait_ge(idx_ready, n + 1 if isinstance(n, int) and n == 0 else n + 2)
                    for h in range(NH):
                        if isinstance(n, int) and n == 0 and h == NH // 2:
                            pool.wait_ge(idx_ready, 2)
                        if not (isinstance(n, int) and n * NH + h < SLOTS):
                            pool.wait_ge(chunk_done, n * NH + (h + 1 - SLOTS))
                        rest(pool, pool_rests)
                        for k in range(K):
                            e = h * K + k
                            pool.indirect_dma_start(
                                out=rows[:, h % SLOTS, k, :], out_offset=None, in_=table_d,
                                in_offset=bass.IndirectOffsetOnAxis(ap=idx[:, par, e:e + 1], axis=0),
                            ).then_inc(gathered[h % SLOTS][k // 4], 16)
                tiles(pool, step)

            @block.tensor
            def _(pe):
                def route(n, par):
                    pe.wait_ge(x2_in[par], 8 * (n - par) + 16)
                    if not (isinstance(n, int) and n < 1):
                        pe.wait_ge(xn_ready, n)
                    for c in range(CC):
                        mm = pe.transpose(ps_xT[:, c, :], x2_tile[:, par, c * P:(c + 1) * P], ident[:, :])
                    mm.then_inc(xT_mm, 1)
                    pe.wait_ge(xn_ready, n + 1)
                    if not (isinstance(n, int) and n < 1):
                        pe.wait_ge(scores_read, n)
                    for s in range(2):
                        for p in range(2):
                            at = HALF * (2 * p + s)
                            for c in range(CC):
                                mm = pe.matmul(ps_score[s][:, HALF * p:HALF * (p + 1)], xnT[:, c, :],
                                               keymap[:, c, at:at + HALF], start=(c == 0), stop=(c == CC - 1))
                        mm.then_inc(score_mm, 1)

                def step(n, par):
                    for h in range(NH):
                        if h == 1 and not (isinstance(n, int) and n == TILES - 1):
                            route(n + 1, 1 - par)
                        if h == 0 and not (isinstance(n, int) and n < 2):
                            pe.wait_ge(sum3_done, n - 1)
                        for k in range(K):
                            if k % 4 == 0:
                                pe.wait_ge(diag_ready, n * (2 * NH) + (2 * h + k // 4 + 1))
                            mm = pe.matmul(ps_out[par], diag[:, h % 2, k, :], rows[:, h % SLOTS, k, C:W2],
                                           start=(h == 0 and k == 0), stop=(h == NH - 1 and k == K - 1))
                        mm.then_inc(chunk_done, 1)
                route(0, 0)
                tiles(pe, step)

            @block.scalar
            def _(act):
                def route(n, par):
                    act.wait_ge(x2_in[par], 8 * (n - par) + 16)
                    if not (isinstance(n, int) and n < 2):
                        act.wait_ge(hid_ready, NH * (n - 1))
                    act.activation(ps_x2[par], x2_tile[:, par], ACT.Copy).then_inc(x2c_ready, 1)
                    act.wait_ge(xT_mm, n + 1)
                    if not (isinstance(n, int) and n < 1):
                        act.wait_ge(score_mm, 2 * n)
                    for c in range(CC):
                        last = act.activation(xnT[:, c, :], ps_xT[:, c, :], ACT.Identity, scale=bn_scale[:, c:c + 1],
                                              bias=bn_shift[:, c:c + 1])
                    last.then_inc(xn_ready, 1)

                def gates(n, par):
                    act.wait_ge(idx_ready, n + 2)
                    if not (isinstance(n, int) and n < 2):
                        act.wait_ge(coef_ready, NH * (n - 1))
                    act.activation(gate[:, par, :], sel[:, :, :].rearrange("p h k -> p (h k)"), ACT.Sigmoid)\
                        .then_inc(gate_ready, 1)

                def gelu(n, par, h):
                    act.wait_ge(hid_ready, n * NH + (h + 1))
                    act.activation(gel[:, par, h * K:(h + 1) * K], hid[:, par, h * K:(h + 1) * K], ACT.Gelu)\
                        .then_inc(gelu_ready, 1)

                def diags(n, par, h):
                    act.wait_ge(coef_ready, n * NH + (h + 1))
                    if not (isinstance(n, int) and n * NH + h < 2):
                        act.wait_ge(chunk_done, n * NH + (h - 1))
                    for k in range(K):
                        last = act.activation(diag[:, h % 2, k, :], ident[:, :], ACT.Copy,
                                              scale=coef[:, par, h * K + k:h * K + k + 1])
                        if k % 4 == 3:
                            last.then_inc(diag_ready, 1)

                def std(n, par):
                    act.wait_ge(var3_ready, n + 1)
                    act.activation(sd3[:, :], mv3[:, 1:2], ACT.Sqrt, bias=eps_col[:, :]).then_inc(std3_ready, 1)
                act.wait_ge(norm_ready, 1)
                route(0, 0)
                gates(0, 0)

                def step(n, par):
                    more = not (isinstance(n, int) and n == TILES - 1)
                    for h in range(NH):
                        gelu(n, par, h)
                        diags(n, par, h)
                        if h == 1:
                            if not (isinstance(n, int) and n < 1):
                                std(n - 1, 1 - par)
                            if more:
                                route(n + 1, 1 - par)
                        if h == ROUTE_AT and more:
                            gates(n + 1, 1 - par)
                tiles(act, step)
                std(TILES - 1, 1)

            @block.vector
            def _(dve):
                def route(n, par):
                    if not (isinstance(n, int) and n < 1):
                        dve.wait_ge(gate_ready, n)
                        parts = [range(NH)]
                    else:
                        parts = [range(NH // 2), range(NH // 2, NH)]
                    for part in parts:
                        best_pairs(n, par, part, part is parts[-1])

                def best_pairs(n, par, part, final):
                    hs = slice(part[0], part[-1] + 1)
                    ks = slice(K * part[0], K * (part[-1] + 1))
                    nh = len(part)
                    nk = nh * K

                    def score(p, h):
                        at = HALF * p + h % (NH // 2) * NK
                        return ps_score[h // (NH // 2)][:, at:at + NK]
                    dve.wait_ge(score_mm, n * 2 + (2 if final else 1))
                    rest(dve, dve_rests)
                    for p in range(2):
                        for h in part:
                            dve.max(out=top[:, p, h, :], in_=score(p, h))
                    dve.drain()
                    for p in range(2):
                        for h in part:
                            last = dve.max_index(out=top_i[:, p, h, :], in_max=top[:, p, h, :], in_values=score(p, h))
                    if final:
                        last.then_inc(scores_read, 1)
                    dve.tensor_tensor(pair[:, hs], top[:, 0, hs, :, None].to_broadcast([P, nh, K, K]),
                                      top[:, 1, hs, None, :].to_broadcast([P, nh, K, K]), ALU.add)
                    dve.drain()
                    for h in part:
                        dve.max(out=sel[:, h, :], in_=pair[:, h, :, :].rearrange("p a b -> p (a b)"))
                    dve.drain()
                    for h in part:
                        dve.max_index(out=sel_i[:, h, :], in_max=sel[:, h, :],
                                      in_values=pair[:, h, :, :].rearrange("p a b -> p (a b)"))
                    dve.drain()
                    flat_i = sel_i[:, hs, :].rearrange("p h k -> p (h k)")
                    dve.tensor_scalar(half_i[:, 0, ks], flat_i, 3, None, ALU.logical_shift_right)
                    dve.tensor_scalar(half_i[:, 1, ks], flat_i, K - 1, None, ALU.bitwise_and)
                    dve.drain()
                    for p in range(2):
                        dve.tensor_tensor(hot[:, p, ks], half_i[:, p, ks, None].to_broadcast([P, nk, K]),
                                          iota8[:, None, :].to_broadcast([P, nk, K]), ALU.is_equal)
                    dve.drain()
                    for p in range(2):
                        h4 = hot[:, p, ks].rearrange("p (h k) j -> p h k j", h=nh)
                        dve.tensor_tensor(h4, h4, top_i[:, p, hs, None, :].to_broadcast([P, nh, K, K]), ALU.mult)
                    dve.drain()
                    for p in range(2):
                        dve.tensor_reduce(half_key[:, p, ks], hot[:, p, ks], AX.X, ALU.add)
                    dve.drain()
                    dve.scalar_tensor_tensor(out=idx[:, par, ks], in0=half_key[:, 0, ks], scalar=float(NK),
                                             in1=half_key[:, 1, ks], op0=ALU.mult, op1=ALU.add).then_inc(idx_ready, 1)

                def hidden(n, par, h):
                    for k in range(K):
                        if k % 4 == 0:
                            dve.wait_ge(gathered[h % SLOTS][k // 4], n * (2 * 16 * 4) + 16 * 4 * (h // SLOTS + 1))
                        last = dve.tensor_tensor_reduce(
                            out=rows[:, h % SLOTS, k, 0:C], in0=rows[:, h % SLOTS, k, 0:C], in1=ps_x2[par],
                            scale=1.0, scalar=0.0, op0=ALU.mult, op1=ALU.add, accum_out=hid[:, par, h * K + k:h * K + k + 1])
                    last.then_inc(hid_ready, 1)

                def coefs(n, par, h):
                    dve.wait_ge(gelu_ready, n * NH + (h + 1))
                    s = slice(h * K, (h + 1) * K)
                    dve.tensor_tensor(coef[:, par, s], gel[:, par, s], gate[:, par, s], ALU.mult)\
                        .then_inc(coef_ready, 1)

                def norm(n, par):
                    dve.wait_ge(chunk_done, NH * (n + 1))
                    dve.tensor_tensor(y3[:, :], ps_out[par], x2_tile[:, par], ALU.add).then_inc(sum3_done, 1)
                    dve.drain()
                    dve.bn_stats(out=st3[:, :], in_=y3[:, :])
                    dve.drain()
                    dve.bn_aggr(out=mv3[:, :], in_=st3[:, :]).then_inc(var3_ready, 1)

                def scale(n, par):
                    dve.wait_ge(std3_ready, n + 1)
                    dve.reciprocal(rs3[:, :], sd3[:, :])
                    dve.drain()
                    if not (isinstance(n, int) and n < 2):
                        dve.wait_ge(y_out[par], 8 * (n - par))
                    dve.tensor_scalar(yo[:, par, :], y3[:, :], mv3[:, 0:1], rs3[:, :], ALU.subtract, ALU.mult)\
                        .then_inc(y_ready, 1)
                route(0, 0)

                def step(n, par):
                    old = not (isinstance(n, int) and n < 1)
                    more = not (isinstance(n, int) and n == TILES - 1)
                    dve.wait_ge(x2c_ready, n + 1)
                    dve.wait_ge(gate_ready, n + 1)
                    for h in range(NH):
                        hidden(n, par, h)
                        coefs(n, par, h)
                        if h == 0 and old:
                            norm(n - 1, 1 - par)
                        if h == 2 and old:
                            scale(n - 1, 1 - par)
                        if h == ROUTE_AT and more:
                            route(n + 1, 1 - par)
                tiles(dve, step)
                norm(TILES - 1, 1)
                scale(TILES - 1, 1)


def kernel(x, ctx_1024, L0_attn_qkv_w, L0_attn_qkv_b, L0_attn_proj_w, L0_attn_proj_b, L0_ffn_bn_gamma,
           L0_ffn_bn_beta, L0_ffn_w_q, L0_ffn_keys_p, L0_ffn_down, L0_ffn_up):
    import numpy as np
    import concourse.bacc as bacc
    from concourse import mybir
    from concourse.bass_utils import run_bass_kernel_spmd as run

    B, T, C = x.shape
    a = lambda v: np.ascontiguousarray(np.asarray(v))
    x, ctx_1024 = a(x), a(ctx_1024)
    hs = L0_attn_qkv_w.shape[0] // 3
    flat = x.reshape(B * T, C)
    kp = a(L0_ffn_keys_p)
    ins = {
        "x": flat,
        "xT": a(flat.T),
        "ctx_rows": ctx_1024,
        "ctx_cols": a(ctx_1024.transpose(2, 0, 1)),
        "wqkvT": a(a(L0_attn_qkv_w).T),
        "bqkv": a(L0_attn_qkv_b).reshape(3 * hs, 1),
        "projT": a(a(L0_attn_proj_w).reshape(C, C // hs, hs).transpose(2, 0, 1)).reshape(hs, C * (C // hs)),
        "projb": a(L0_attn_proj_b).reshape(1, C),
        "gamma": a(a(L0_ffn_bn_gamma).reshape(C // 128, 128).T),
        "beta": a(a(L0_ffn_bn_beta).reshape(C // 128, 128).T),
        "wq": a(L0_ffn_w_q),
        "keysT": a(kp.transpose(3, 2, 0, 1)).reshape(kp.shape[3], 2 * kp.shape[0], kp.shape[1]),
        "table": np.concatenate([a(L0_ffn_down), a(L0_ffn_up)], axis=1),
    }
    nc = bacc.Bacc("TRN2", target_bir_lowering=False, num_devices=1)
    arrays, args = {}, []
    for name, v in ins.items():
        arrays[f"in_{name}"] = v
        args.append(nc.dram_tensor(f"in_{name}", v.shape, mybir.dt.from_np(v.dtype), kind="ExternalInput").ap())
    args.append(nc.dram_tensor("out_y", (B * T, C), mybir.dt.float32, kind="ExternalOutput").ap())
    decoder_layer(nc, *args)
    r = run(nc, [arrays], core_ids=[0])
    return r.results[0]["out_y"].reshape(B, T, C)
```
